# Optimizing a Trainium2 kernel written in Bass

```python
import numpy as np
import jax
import jax.numpy as jnp

def _softmax(x, axis=-1):
    return jax.nn.softmax(x, axis=axis)

def _gelu(x):
    return jax.nn.gelu(x, approximate=True)

def _silu(x):
    return jax.nn.silu(x)

def _sigmoid(x):
    return jax.nn.sigmoid(x)

def _layernorm(x, axis=-1, eps=1e-05):
    m = jnp.mean(x, axis=axis, keepdims=True)
    v = jnp.var(x, axis=axis, keepdims=True)
    return (x - m) / jnp.sqrt(v + eps)

def _scatter_add(tgt, idx, src, axis=0):
    return tgt.at[idx].add(src)

def _segment_sum(src, seg, n):
    return jax.ops.segment_sum(src, seg, n)
kernel_name = 'mk_macaron_d1_jaxref_r8_cac156'

def setup_inputs(seed: int=0):
    np.random.seed(seed)
    _w = jnp.asarray

    def _L0_attn_setup():
        import jax, jax.numpy as jnp
        import numpy as np
        B, M, D, H, K, V = (4, 256, 128, 16, 64, 64)
        key = jax.random.key(seed)
        ks = jax.random.split(key, 5)
        return {'x': jax.random.normal(ks[0], (B, M, D), dtype=jnp.float32), 'P_q': jax.random.normal(ks[1], (H, D, K), dtype=jnp.float32) * 0.02, 'P_k': jax.random.normal(ks[2], (H, D, K), dtype=jnp.float32) * 0.02, 'P_v': jax.random.normal(ks[3], (H, D, V), dtype=jnp.float32) * 0.02, 'P_o': jax.random.normal(ks[4], (H, D, V), dtype=jnp.float32) * 0.02}
    _L0_attn_in = _L0_attn_setup()

    def _L0_ffn_setup():
        import jax, jax.numpy as jnp
        import numpy as np
        B, S, H = (2, 256, 128)
        E, F, K = (64, 64, 8)
        G, TG = (8, 4)
        SCALE = 2.5
        F_SH = 64

        def _gate(x, gate_w, gate_bias):
            scores = jax.nn.sigmoid(x @ gate_w.T)
            sc = scores + gate_bias[None, :]
            T = x.shape[0]
            group_scores = jax.lax.top_k(sc.reshape(T, G, E // G), 2)[0].sum(-1)
            _, gidx = jax.lax.top_k(group_scores, TG)
            gmask = jnp.zeros((T, G), sc.dtype).at[jnp.arange(T)[:, None], gidx].set(1.0)
            smask = jnp.repeat(gmask, E // G, axis=1)
            masked = jnp.where(smask > 0, sc, -jnp.inf)
            _, tidx = jax.lax.top_k(masked, K)
            tw = jnp.take_along_axis(scores, tidx, axis=1)
            tw = tw / (tw.sum(-1, keepdims=True) + 1e-20)
            return (tidx, tw * SCALE)
        key = jax.random.key(seed)
        ks = jax.random.split(key, 9)

        def w(k, shape, fan_in):
            return jax.random.normal(k, shape, jnp.float32) / np.float32(np.sqrt(fan_in))
        return {'hidden_states': jax.random.normal(ks[0], (B, S, H), jnp.float32), 'gate_w': w(ks[1], (E, H), H), 'gate_bias': jax.random.normal(ks[2], (E,), jnp.float32) * 0.01, 'We_gate': w(ks[3], (E, H, F), H), 'We_up': w(ks[4], (E, H, F), H), 'We_down': w(ks[5], (E, F, H), F), 'Ws_gate': w(ks[6], (H, F_SH), H), 'Ws_up': w(ks[7], (H, F_SH), H), 'Ws_down': w(ks[8], (F_SH, H), F_SH)}
    _L0_ffn_in = _L0_ffn_setup()
    _d = {'L0_attn_x': _L0_attn_in['x'], 'L0_attn_P_q': _L0_attn_in['P_q'], 'L0_attn_P_k': _L0_attn_in['P_k'], 'L0_attn_P_v': _L0_attn_in['P_v'], 'L0_attn_P_o': _L0_attn_in['P_o'], 'L0_ffn_gate_w': _L0_ffn_in['gate_w'], 'L0_ffn_gate_bias': _L0_ffn_in['gate_bias'], 'L0_ffn_We_gate': _L0_ffn_in['We_gate'], 'L0_ffn_We_up': _L0_ffn_in['We_up'], 'L0_ffn_We_down': _L0_ffn_in['We_down'], 'L0_ffn_Ws_gate': _L0_ffn_in['Ws_gate'], 'L0_ffn_Ws_up': _L0_ffn_in['Ws_up'], 'L0_ffn_Ws_down': _L0_ffn_in['Ws_down']}
    _x0 = _d['L0_attn_x']
    _d['L0_attn_x'] = jax.random.normal(jax.random.fold_in(jax.random.key(seed), 1), (16, 256, 128), dtype=_x0.dtype)
    del _x0
    return _d

def reference(L0_attn_x, L0_attn_P_q, L0_attn_P_k, L0_attn_P_v, L0_attn_P_o, L0_ffn_gate_w, L0_ffn_gate_bias, L0_ffn_We_gate, L0_ffn_We_up, L0_ffn_We_down, L0_ffn_Ws_gate, L0_ffn_Ws_up, L0_ffn_Ws_down):

    def _L0_attn_ref(x, P_q, P_k, P_v, P_o):
        import jax, jax.numpy as jnp
        import numpy as np
        B, M, D, H, K, V = (4, 256, 128, 16, 64, 64)
        Q = jnp.einsum('bmd,hdk->bhmk', x, P_q)
        Kt = jnp.einsum('bmd,hdk->bhmk', x, P_k)
        Vt = jnp.einsum('bmd,hdv->bhmv', x, P_v)
        scale = 1.0 / jnp.sqrt(jnp.asarray(K, dtype=x.dtype))
        logits = jnp.einsum('bhmk,bhnk->bhmn', Q, Kt) * scale
        m = logits.shape[-1]
        causal = jnp.tril(jnp.ones((m, m), dtype=bool))
        logits = jnp.where(causal[None, None], logits, jnp.asarray(-jnp.inf, dtype=logits.dtype))
        weights = jax.nn.softmax(logits, axis=-1)
        o = jnp.einsum('bhmn,bhnv->bhmv', weights, Vt)
        y = jnp.einsum('bhmv,hdv->bmd', o, P_o)
        return y

    def _L0_ffn_ref(hidden_states, gate_w, gate_bias, We_gate, We_up, We_down, Ws_gate, Ws_up, Ws_down):
        import jax, jax.numpy as jnp
        import numpy as np
        B, S, H = (2, 256, 128)
        E, F, K = (64, 64, 8)
        G, TG = (8, 4)
        SCALE = 2.5
        F_SH = 64

        def _gate(x, gate_w, gate_bias):
            scores = jax.nn.sigmoid(x @ gate_w.T)
            sc = scores + gate_bias[None, :]
            T = x.shape[0]
            group_scores = jax.lax.top_k(sc.reshape(T, G, E // G), 2)[0].sum(-1)
            _, gidx = jax.lax.top_k(group_scores, TG)
            gmask = jnp.zeros((T, G), sc.dtype).at[jnp.arange(T)[:, None], gidx].set(1.0)
            smask = jnp.repeat(gmask, E // G, axis=1)
            masked = jnp.where(smask > 0, sc, -jnp.inf)
            _, tidx = jax.lax.top_k(masked, K)
            tw = jnp.take_along_axis(scores, tidx, axis=1)
            tw = tw / (tw.sum(-1, keepdims=True) + 1e-20)
            return (tidx, tw * SCALE)
        b, s, h = hidden_states.shape
        x = hidden_states.reshape(-1, h).astype(jnp.float32)
        tidx, tw = _gate(x, gate_w, gate_bias)
        T = x.shape[0]
        w_dense = jnp.zeros((T, E), tw.dtype).at[jnp.arange(T)[:, None], tidx].add(tw)

        def body(acc, ws):
            wg, wu, wdn, cw = ws
            hmid = jax.nn.silu(x @ wg) * (x @ wu)
            return (acc + cw[:, None] * (hmid @ wdn), None)
        y, _ = jax.lax.scan(body, jnp.zeros_like(x), (We_gate, We_up, We_down, w_dense.T))
        y = y.reshape(b, s, h)
        shared = jax.nn.silu(hidden_states @ Ws_gate) * (hidden_states @ Ws_up) @ Ws_down
        return y + shared
    x = L0_attn_x
    x = x + 0.5 * _L0_ffn_ref(_layernorm(x, axis=-1), L0_ffn_gate_w, L0_ffn_gate_bias, L0_ffn_We_gate, L0_ffn_We_up, L0_ffn_We_down, L0_ffn_Ws_gate, L0_ffn_Ws_up, L0_ffn_Ws_down)
    x = x + _L0_attn_ref(_layernorm(x, axis=-1), L0_attn_P_q, L0_attn_P_k, L0_attn_P_v, L0_attn_P_o)
    x = x + 0.5 * _L0_ffn_ref(_layernorm(x, axis=-1), L0_ffn_gate_w, L0_ffn_gate_bias, L0_ffn_We_gate, L0_ffn_We_up, L0_ffn_We_down, L0_ffn_Ws_gate, L0_ffn_Ws_up, L0_ffn_Ws_down)
    return x

_drawn_inputs = setup_inputs


def setup_inputs(seed=0):
    import zlib

    import numpy as np

    out = dict(_drawn_inputs(seed))
    spreads = {}
    factors = {'L0_attn_P_q': 6.67, 'L0_attn_P_k': 8.0}
    for name, (base, spread) in spreads.items():
        noise = np.random.default_rng([zlib.crc32(name.encode()), seed]).standard_normal(out[name].shape)
        drawn = base * np.exp(spread * noise) if base else spread * noise
        out[name] = jnp.asarray(drawn.astype(out[name].dtype))
    for name, factor in factors.items():
        out[name] = (out[name] * factor).astype(out[name].dtype)
    return out
```

```python
from contextlib import ExitStack

import concourse.bass as bass
from concourse import mybir

F32 = mybir.dt.float32
F32R = mybir.dt.float32r
BF16 = mybir.dt.bfloat16
ALU = mybir.AluOpType
ACT = mybir.ActivationFunctionType
AX_X = mybir.AxisListType.X

P = 128
D = 128
E = 64
F = 64
NG = 8
TOPK_GROUPS = 4
PAIRS = E // 2
SLOTS = PAIRS + 1
H = 16
HD = 64
SEQ = 256
CT = 4
CHUNK = CT * P
SCALE = 2.5
LN_EPS = 1e-5
OFF = -3.0e38
TAKEN = -3.3e38
MASKED = -1.0e30
LEAD_F = 5
LEAD_A = 3


def setup(nc, w, x, x_all, dr, psum):
    SW = 1024
    with ExitStack() as ctx:
        def sb(name, shape, dt=F32):
            return ctx.enter_context(nc.sbuf_tensor(name, shape, dt))

        def sem(name):
            return ctx.enter_context(nc.semaphore(name))

        NST = 6
        stage = sb("stage", [P, NST, SW])
        po_raw = sb("po_raw", [P, H * HD])
        gw_raw = sb("gw_raw", [E, D])
        sel_raw = sb("sel_raw", [P, SW])
        mask_raw = sb("mask_raw", [P, 2, P])
        landed = [sem(f"landed{i}") for i in range(NST)]
        x_landed, small_landed = sem("x_landed"), sem("small_landed")
        hi_split, lo_split = sem("hi_split"), sem("lo_split")
        const_step, ident_ready = sem("const_step"), sem("ident_ready")
        sel_step, sel_copied = sem("sel_step"), sem("sel_copied")
        turned, turned_copied, gw_hi = sem("turned"), sem("turned_copied"), sem("gw_hi")

        pieces = []
        for j in range(4):
            n = SW // F
            for kind in ("wg", "wu"):
                c = slice(j * SW, (j + 1) * SW)
                pieces.append((w[kind + "_hi"][:, c], w[kind + "_lo"][:, c],
                               dr[kind][j * n:(j + 1) * n].rearrange("e d f -> d e f"), (P, n, F)))
            n = SW // D
            c = slice(j * SW, (j + 1) * SW)
            pieces.append((w["wd_hi"][:, c], w["wd_lo"][:, c],
                           dr["wd"][2 * j * n:2 * (j + 1) * n].rearrange("(n t) f h -> (t f) n h", t=2), (P, n, D)))
        for kind, src in (("wg", "sg"), ("wu", "su")):
            c = slice(PAIRS * P, PAIRS * P + F)
            pieces.append((w[kind + "_hi"][:, c], w[kind + "_lo"][:, c], dr[src], (P, F)))
        c = slice(PAIRS * P, PAIRS * P + D)
        pieces.append((w["wd_hi"][0:F, c], w["wd_lo"][0:F, c], dr["sd"], (F, D)))
        for kind in ("pq", "pk", "pv"):
            pieces.append((w[kind + "_hi"][:, :], w[kind + "_lo"][:, :],
                           dr[kind].rearrange("h d k -> d h k"), (P, H, HD)))

        def staged(n):
            shape = pieces[n][3]
            cols = shape[1] * (shape[2] if len(shape) == 3 else 1)
            return stage[0:shape[0], n % NST, 0:cols]

        block = ctx.enter_context(nc.Block())

        @block.sync
        def _(sp):
            for n, (_, _, src, shape) in enumerate(pieces):
                if n >= NST:
                    sp.wait_ge(lo_split, n - NST + 1)
                dst = staged(n)
                if len(shape) == 3:
                    dst = dst.rearrange("p (a b) -> p a b", b=shape[2])
                sp.dma_start(dst, src).then_inc(landed[n % NST], 16)

        @block.gpsimd
        def _(pool):
            nc.gpsimd.memset(w["ident"][:, :], 0.0).then_inc(const_step, 1)
            nc.gpsimd.memset(mask_raw[:, :, :], 0.0).then_inc(const_step, 1)
            pool.wait_ge(const_step, 2)
            nc.gpsimd.affine_select(out=w["ident"][:, :], in_=w["ident"][:, :], compare_op=ALU.not_equal,
                                    fill=1.0, base=0, pattern=[[-1, P]], channel_multiplier=1).then_inc(ident_ready, 1)
            nc.gpsimd.affine_select(out=mask_raw[:, :, :], in_=mask_raw[:, :, :], compare_op=ALU.is_ge,
                                    fill=MASKED, base=0, pattern=[[0, 2], [-1, P]],
                                    channel_multiplier=1).then_inc(ident_ready, 1)
            nc.gpsimd.memset(w["earlier"][:, :], 1.0).then_inc(const_step, 1)
            pool.wait_ge(const_step, 3)
            earlier = w["earlier"][:, :].rearrange("p (g h) -> p g h", h=NG)
            nc.gpsimd.affine_select(out=earlier, in_=earlier, compare_op=ALU.is_gt, fill=0.0, base=0,
                                    pattern=[[1, NG], [-1, NG]], channel_multiplier=0).then_inc(const_step, 1)
            nc.gpsimd.memset(w["minus_half"][:, :], -0.5).then_inc(const_step, 1)
            nc.gpsimd.memset(w["eps"][:, :], LN_EPS).then_inc(const_step, 1)
            for kind in ("gw_hi", "gw_lo"):
                nc.gpsimd.memset(w[kind][:, E:P].bitcast(F32), 0.0).then_inc(const_step, 1)
            for kind in ("wg_hi", "wg_lo", "wu_hi", "wu_lo"):
                nc.gpsimd.memset(w[kind][:, PAIRS * P + F:SLOTS * P].bitcast(F32), 0.0).then_inc(const_step, 1)
            for j in range(4):
                n = SW // P
                v = sel_raw[:, :].rearrange("p (n t c) -> p n t c", t=2, c=F)
                if j >= 1:
                    pool.wait_ge(sel_copied, j)
                nc.gpsimd.memset(sel_raw[:, :], 0.0).then_inc(sel_step, 1)
                for half in range(2):
                    pool.wait_ge(sel_step, 3 * j + half + 1)
                    nc.gpsimd.affine_select(out=v, in_=v, compare_op=ALU.not_equal, fill=1.0,
                                            base=-(half * E + 2 * j * n), pattern=[[-2, n], [-1, 2], [0, F]],
                                            channel_multiplier=1).then_inc(sel_step, 1)

        @block.scalar
        def _(act):
            act.dma_start(x_all[:, 0:CT, :], x[:, 0:CT, :]).then_inc(x_landed, 16)
            act.dma_start(gw_raw[:, :], dr["gw"]).then_inc(small_landed, 16)
            act.dma_start(w["bias"][:, :], dr["gb"]).then_inc(small_landed, 16)
            act.dma_start(po_raw[:, :].rearrange("d (h v) -> d h v", v=HD),
                          dr["po"].rearrange("h d v -> d h v")).then_inc(small_landed, 16)
            act.dma_start(x_all[:, CT:, :], x[:, CT:, :]).then_inc(x_landed, 16)
            act.wait_ge(ident_ready, 2)
            nc.scalar.copy(w["mask"][:, :], mask_raw[:, :, :].rearrange("p a b -> p (a b)"))
            nc.scalar.copy(w["ident_b"][:, :], w["ident"][:, :])
            act.wait_ge(turned, 1)
            nc.scalar.copy(w["gw_hi"][:, 0:E], psum[2][:, 0:E]).then_inc(gw_hi, 1)
            for j in range(4):
                act.wait_ge(sel_step, 3 * j + 3)
                nc.scalar.copy(w["sel"][:, j * SW:(j + 1) * SW], sel_raw[:, :]).then_inc(sel_copied, 1)
            for n, (hi, _, _, _) in enumerate(pieces):
                act.wait_ge(landed[n % NST], 16 * (n // NST + 1))
                nc.scalar.copy(hi, staged(n)).then_inc(hi_split, 1)
            act.wait_ge(x_landed, 32)

        @block.vector
        def _(dve):
            for kind in ("wd_hi", "wd_lo"):
                nc.vector.memset(w[kind][F:P, PAIRS * P:SLOTS * P].bitcast(F32), 0.0)
            dve.wait_ge(gw_hi, 1)
            nc.vector.tensor_tensor(w["gw_lo"][:, 0:E], psum[2][:, 0:E], w["gw_hi"][:, 0:E].bitcast(F32),
                                    ALU.subtract)
            for b in range(2):
                dve.wait_ge(turned, b + 2)
                nc.vector.tensor_copy(w["po"][:, 4 * b * P:4 * (b + 1) * P], psum[b][:, :])
            for n, (hi, lo, _, _) in enumerate(pieces):
                dve.wait_ge(hi_split, n + 1)
                nc.vector.tensor_tensor(lo, staged(n), hi.bitcast(F32), ALU.subtract).then_inc(lo_split, 1)

        @block.tensor
        def _(pe):
            pe.wait_ge(ident_ready, 1)
            pe.wait_ge(small_landed, 48)
            nc.tensor.transpose(psum[2][:, 0:E], gw_raw[:, :], w["ident"][0:E, 0:E]).then_inc(turned, 1)
            for b in range(2):
                for j in range(4):
                    mm = nc.tensor.transpose(psum[b][:, j * P:(j + 1) * P],
                                             po_raw[:, (4 * b + j) * P:(4 * b + j + 1) * P], w["ident"][:, :])
                mm.then_inc(turned, 1)


def ffn(nc, tag, w, x_all, psum, out):
    NC = x_all.shape[1] // CT
    gate_bank, up_bank, mix_bank = psum[0:2], psum[2:4], psum[4:6]
    acc, misc = psum[6], psum[7]
    with ExitStack() as ctx:
        def sb(name, shape, dt=F32):
            return ctx.enter_context(nc.sbuf_tensor(tag + name, shape, dt))

        def sem(name):
            return ctx.enter_context(nc.semaphore(tag + name))

        xn = sb("xn", [P, CT, D])
        stats = sb("stats", [P, CT, 6])
        moments = sb("moments", [P, CT, 2])
        veps = sb("veps", [P, CT])
        rstd = sb("rstd", [P, CT])
        hold = sb("hold", [P, 1])
        xT_hi = sb("xT_hi", [P, 2 * CHUNK], F32R)
        xT_lo = sb("xT_lo", [P, 2 * CHUNK], F32R)
        mixT = sb("mixT", [P, 2 * CHUNK], F32R)
        hid = sb("hid", [P, 3, CHUNK])
        hid_hi = sb("hid_hi", [P, 3, CHUNK], F32R)
        hid_lo = sb("hid_lo", [P, 3, CHUNK], F32R)
        yT = sb("yT", [P, CHUNK])
        score = sb("score", [P, CT * E])
        biased = sb("biased", [P, CT * E])
        kept = sb("kept", [P, CT * E])
        chosen = sb("chosen", [P, CT * E])
        mix = sb("mix", [P, CT, 2, E])
        h4, l4 = sb("h4", [P, CT * NG, 4]), sb("l4", [P, CT * NG, 4])
        h2, m2, l2 = (sb(n, [P, CT * NG, 2]) for n in ("h2", "m2", "l2"))
        h1, m1, l1 = (sb(n, [P, CT * NG]) for n in ("h1", "m1", "l1"))
        gscore, rank, keep, drop = (sb(n, [P, CT * NG]) for n in ("gscore", "rank", "keep", "drop"))
        top8 = sb("top8", [P, CT, 8])
        total, inv = sb("total", [P, CT]), sb("inv", [P, CT])

        gate_done, up_done, mix_done, down_done = sem("gate_done"), sem("up_done"), sem("mix_done"), sem("down_done")
        silu_done, gated, weighted = sem("silu_done"), sem("gated"), sem("weighted")
        hid_hi_done, hid_lo_done = sem("hid_hi_done"), sem("hid_lo_done")
        yT_done, y_turned, x_updated = sem("yT_done"), sem("y_turned"), sem("x_updated")
        ln_step, rstd_step, xn_turned = sem("ln_step"), sem("rstd_step"), sem("xn_turned")
        xT_hi_done, xT_lo_done = sem("xT_hi_done"), sem("xT_lo_done")
        logits_done, score_done, route_step = sem("logits_done"), sem("score_done"), sem("route_step")
        mix_turned, mixT_done, stored = sem("mix_turned"), sem("mixT_done"), sem("stored")

        LN_STEPS = 3
        ROUTE_STEPS = 26

        def place(c, q):
            return (c, q) if q < SLOTS else (c + 1, q - SLOTS)

        def tiles(c):
            return slice(c * CT, (c + 1) * CT) if isinstance(c, int) else bass.ds(c * CT, CT)

        def half(c, width):
            o = (c % 2) * width
            return slice(o, o + width) if isinstance(c, int) else bass.ds(o, width)

        def body(engine_slot, c, last):
            for q in range(LEAD_F, SLOTS + LEAD_F):
                if not last or q < SLOTS + 4:
                    engine_slot(c, q, last)

        def run(engine, engine_slot):
            for q in range(LEAD_F):
                engine_slot(0, q, False)
            with engine.Fori(0, NC - 1) as c:
                body(engine_slot, c, False)
            body(engine_slot, NC - 1, True)

        block = ctx.enter_context(nc.Block())

        @block.tensor
        def _(pe):
            def turn_xn(n):
                pe.wait_ge(ln_step, LN_STEPS * n + 3)
                for j in range(CT):
                    mm = nc.tensor.transpose(misc[:, j * P:(j + 1) * P], xn[:, j, :], w["ident"][:, :])
                mm.then_inc(xn_turned, 1)

            def logits(n):
                pe.wait_ge(xT_lo_done, n + 1)
                for a, (wk, xt) in enumerate((("gw_hi", xT_hi), ("gw_lo", xT_hi), ("gw_hi", xT_lo))):
                    mm = nc.tensor.matmul(misc[:, :], w[wk][:, :], xt[:, half(n, CHUNK)],
                                          start=(a == 0), stop=(a == 2))
                mm.then_inc(logits_done, 1)

            def turn_logits(n):
                pe.wait_ge(score_done, 2 * n + 1)
                for j in range(CT):
                    mm = nc.tensor.transpose(misc[:, j * P:(j + 1) * P], yT[:, j * P:(j + 1) * P], w["ident"][:, :])
                mm.then_inc(logits_done, 1)

            def turn_mix(n):
                pe.wait_ge(route_step, ROUTE_STEPS * (n + 1))
                pe.wait_ge(score_done, 2 * n + 2)
                for j in range(CT):
                    mm = nc.tensor.transpose(misc[:, j * P:(j + 1) * P],
                                             mix[:, j, :, :].rearrange("p a b -> p (a b)"), w["ident"][:, :])
                mm.then_inc(mix_turned, 1)

            def three(bank, kind, p, rhs_hi, rhs_lo, start=True, stop=True):
                hi, lo = w[kind + "_hi"][:, p * P:(p + 1) * P], w[kind + "_lo"][:, p * P:(p + 1) * P]
                nc.tensor.matmul(bank[:, :], hi, rhs_hi, start=start, stop=False)
                nc.tensor.matmul(bank[:, :], lo, rhs_hi, start=False, stop=False)
                return nc.tensor.matmul(bank[:, :], hi, rhs_lo, start=False, stop=stop)

            def up(c, p):
                first = isinstance(c, int) and c == 0
                xh, xl = xT_hi[:, half(c, CHUNK)], xT_lo[:, half(c, CHUNK)]
                if p == 0:
                    pe.wait_ge(xT_lo_done, c + 1)
                if p == PAIRS:
                    g, u = mix_bank
                    pe.wait_ge(weighted, PAIRS * c + PAIRS - 1)
                else:
                    g, u = gate_bank[p % 2], up_bank[p % 2]
                    if p >= 2:
                        pe.wait_ge(silu_done, SLOTS * c + p - 1)
                    elif not first:
                        pe.wait_ge(silu_done, SLOTS * c + p - 2)
                three(g, "wg", p, xh, xl).then_inc(gate_done, 1)
                if p == PAIRS:
                    pe.wait_ge(weighted, PAIRS * c + PAIRS)
                elif p >= 2:
                    pe.wait_ge(gated, SLOTS * c + p - 1)
                elif not first:
                    pe.wait_ge(gated, SLOTS * c + p - 2)
                three(u, "wu", p, xh, xl).then_inc(up_done, 1)
                if p == PAIRS:
                    return
                if p == 0:
                    pe.wait_ge(mixT_done, c + 1)
                if p >= 2:
                    pe.wait_ge(weighted, PAIRS * c + p - 1)
                elif not first:
                    pe.wait_ge((silu_done, gated)[p], SLOTS * c)
                nc.tensor.matmul(mix_bank[p % 2][:, :], w["sel"][:, p * P:(p + 1) * P], mixT[:, half(c, CHUNK)],
                                 start=True, stop=True).then_inc(mix_done, 1)

            def down(c, p):
                pe.wait_ge(hid_lo_done, SLOTS * c + p + 1)
                if p == 0 and not (isinstance(c, int) and c == 0):
                    pe.wait_ge(yT_done, c)
                three(acc, "wd", p, hid_hi[:, p % 3, :], hid_lo[:, p % 3, :],
                      start=(p == 0), stop=(p == PAIRS)).then_inc(down_done, 1)

            def turn_y(c, last):
                pe.wait_ge(yT_done, c + 1)
                pe.wait_ge(mixT_done, c + 1 if last else c + 2)
                for j in range(CT):
                    mm = nc.tensor.transpose(misc[:, j * P:(j + 1) * P], yT[:, j * P:(j + 1) * P], w["ident"][:, :])
                mm.then_inc(y_turned, 1)

            def slot(c, q, last):
                if q < SLOTS or not last:
                    up(*place(c, q))
                if 2 <= q < SLOTS + 2 or (q >= SLOTS + 2 and not last):
                    down(*place(c, q - 2))
                if not last and q >= LEAD_F:
                    if q == 9:
                        turn_xn(c + 1)
                    if q == 11:
                        logits(c + 1)
                    if q == 13:
                        turn_logits(c + 1)
                    if q == 29:
                        turn_mix(c + 1)
                if q == SLOTS + 3:
                    turn_y(c, last)

            turn_xn(0)
            logits(0)
            turn_logits(0)
            turn_mix(0)
            run(pe, slot)

        @block.scalar
        def _(act):
            def xT_high(n):
                act.wait_ge(xn_turned, n + 1)
                nc.scalar.copy(xT_hi[:, half(n, CHUNK)], misc[:, :]).then_inc(xT_hi_done, 1)

            def sigmoid(n):
                act.wait_ge(logits_done, 2 * n + 1)
                nc.scalar.activation(yT[:, :], misc[:, :], ACT.Sigmoid).then_inc(score_done, 1)

            def copy_score(n):
                act.wait_ge(logits_done, 2 * n + 2)
                if not (isinstance(n, int) and n == 0):
                    act.wait_ge(route_step, ROUTE_STEPS * n)
                nc.scalar.copy(score[:, :].rearrange("p (t e) -> p t e", e=E),
                               misc[:, :].rearrange("p (t n) -> p t n", n=P)[:, :, 0:E]).then_inc(score_done, 1)

            def copy_mixT(n):
                act.wait_ge(mix_turned, n + 1)
                nc.scalar.copy(mixT[:, half(n, CHUNK)], misc[:, :]).then_inc(mixT_done, 1)

            def silu(c, p):
                act.wait_ge(gate_done, SLOTS * c + p + 1)
                if p >= 3 or not (isinstance(c, int) and c == 0):
                    act.wait_ge(hid_lo_done, SLOTS * c + p - 2)
                bank = mix_bank[0] if p == PAIRS else gate_bank[p % 2]
                nc.scalar.activation(hid[:, p % 3, :], bank[:, :], ACT.Silu).then_inc(silu_done, 1)

            def high(c, p):
                if p == PAIRS:
                    act.wait_ge(gated, SLOTS * (c + 1))
                else:
                    act.wait_ge(weighted, PAIRS * c + p + 1)
                if p >= 3 or not (isinstance(c, int) and c == 0):
                    act.wait_ge(down_done, SLOTS * c + p - 2)
                nc.scalar.copy(hid_hi[:, p % 3, :], hid[:, p % 3, :]).then_inc(hid_hi_done, 1)

            def copy_y(c):
                act.wait_ge(down_done, SLOTS * (c + 1))
                nc.scalar.mul(yT[:, :], acc[:, :], 0.5).then_inc(yT_done, 1)

            def slot(c, q, last):
                if q == SLOTS + 2:
                    copy_y(c)
                if q < SLOTS or not last:
                    silu(*place(c, q))
                if 1 <= q < SLOTS + 1 or (q >= SLOTS + 1 and not last):
                    high(*place(c, q - 1))
                if not last and q >= LEAD_F:
                    if q == 9:
                        xT_high(c + 1)
                    if q == 11:
                        sigmoid(c + 1)
                    if q == 13:
                        copy_score(c + 1)
                    if q == 30:
                        copy_mixT(c + 1)

            xT_high(0)
            sigmoid(0)
            copy_score(0)
            copy_mixT(0)
            run(act, slot)

        @block.vector
        def _(dve):
            def v8(t):
                return t[:, :].rearrange("p (g e) -> p g e", e=E // NG)

            def by_tile(t, n):
                return t[:, :].rearrange("p (t n) -> p t n", n=n)

            def ln_moments(n):
                if not (isinstance(n, int) and n == 0):
                    dve.wait_ge(rstd_step, 2 * n)
                for j in range(CT):
                    i = nc.vector.bn_stats(stats[:, j, :], x_all[:, tiles(n), :][:, j, :])
                i.then_inc(ln_step, 1)
                dve.wait_ge(ln_step, LN_STEPS * n + 1)
                nc.vector.memset(hold[:, :], 0.0)
                for j in range(CT):
                    i = nc.vector.bn_aggr(moments[:, j, :], stats[:, j, :])
                i.then_inc(ln_step, 1)

            def ln_apply(n):
                dve.wait_ge(rstd_step, 2 * n + 2)
                dve.wait_ge(xn_turned, n)
                for j in range(CT):
                    i = nc.vector.tensor_scalar(xn[:, j, :], x_all[:, tiles(n), :][:, j, :], moments[:, j, 0:1],
                                                rstd[:, j:j + 1], ALU.subtract, ALU.mult)
                i.then_inc(ln_step, 1)

            def xT_low(n):
                dve.wait_ge(xT_hi_done, n + 1)
                nc.vector.tensor_tensor(xT_lo[:, half(n, CHUNK)], misc[:, :],
                                        xT_hi[:, half(n, CHUNK)].bitcast(F32), ALU.subtract).then_inc(xT_lo_done, 1)

            def route(n, part):
                base = {0: 0, 1: 6, 2: 12, 3: 18, 4: 21, 5: 24}[part]
                done = [base]

                def step(ins):
                    ins.then_inc(route_step, 1)
                    done[0] += 1

                def settled():
                    dve.wait_ge(route_step, ROUTE_STEPS * n + done[0])

                tt, V = nc.vector.tensor_tensor, nc.vector
                G8 = [P, CT, NG, NG]
                gs = by_tile(gscore, NG)
                if part == 0:
                    dve.wait_ge(score_done, 2 * n + 2)
                    dve.wait_ge(mix_turned, n)
                    step(tt(by_tile(biased, E), by_tile(score, E),
                            w["bias"][:, :].rearrange("p (a e) -> p a e", a=1).to_broadcast([P, CT, E]), ALU.add))
                    settled()
                    b = v8(biased)
                    tt(h4[:, :, :], b[:, :, 0:4], b[:, :, 4:8], ALU.max)
                    step(tt(l4[:, :, :], b[:, :, 0:4], b[:, :, 4:8], ALU.min))
                    settled()
                    tt(h2[:, :, :], h4[:, :, 0:2], h4[:, :, 2:4], ALU.max)
                    tt(m2[:, :, :], h4[:, :, 0:2], h4[:, :, 2:4], ALU.min)
                    step(tt(l2[:, :, :], l4[:, :, 0:2], l4[:, :, 2:4], ALU.max))
                    settled()
                    step(tt(l2[:, :, :], l2[:, :, :], m2[:, :, :], ALU.max))
                    settled()
                    tt(h1[:, :], h2[:, :, 0], h2[:, :, 1], ALU.max)
                    tt(m1[:, :], h2[:, :, 0], h2[:, :, 1], ALU.min)
                    step(tt(l1[:, :], l2[:, :, 0], l2[:, :, 1], ALU.max))
                    settled()
                    step(tt(l1[:, :], l1[:, :], m1[:, :], ALU.max))
                elif part == 1:
                    settled()
                    step(tt(gscore[:, :], h1[:, :], l1[:, :], ALU.add))
                    settled()
                    other = gs.rearrange("p t (a g) -> p t a g", a=1).to_broadcast(G8)
                    own = gs.rearrange("p t (g a) -> p t g a", a=1).to_broadcast(G8)
                    beats = kept[:, :].rearrange("p (t g h) -> p t g h", t=CT, g=NG)
                    ties = chosen[:, :].rearrange("p (t g h) -> p t g h", t=CT, g=NG)
                    tt(beats, other, own, ALU.is_gt)
                    step(tt(ties, other, own, ALU.is_equal))
                    settled()
                    step(tt(by_tile(chosen, E), by_tile(chosen, E),
                            w["earlier"][:, :].rearrange("p (a e) -> p a e", a=1).to_broadcast([P, CT, E]), ALU.mult))
                    settled()
                    step(tt(kept[:, :], kept[:, :], chosen[:, :], ALU.add))
                    settled()
                    step(V.tensor_reduce(rank[:, :], v8(kept), AX_X, ALU.add))
                    settled()
                    step(V.tensor_scalar(keep[:, :], rank[:, :], float(TOPK_GROUPS), None, ALU.is_lt))
                elif part == 2:
                    settled()
                    step(V.tensor_scalar(drop[:, :], keep[:, :], -OFF, OFF, ALU.mult, ALU.add))
                    settled()
                    keep_b = keep[:, :].rearrange("p (g a) -> p g a", a=1).to_broadcast([P, CT * NG, E // NG])
                    drop_b = drop[:, :].rearrange("p (g a) -> p g a", a=1).to_broadcast([P, CT * NG, E // NG])
                    step(tt(v8(kept), v8(biased), keep_b, ALU.mult))
                    settled()
                    step(tt(v8(kept), v8(kept), drop_b, ALU.add))
                    settled()
                    V.memset(hold[:, :], 0.0)
                    for j in range(CT):
                        i = V.max(top8[:, j, :], kept[:, j * E:(j + 1) * E])
                    step(i)
                    settled()
                    V.memset(hold[:, :], 0.0)
                    for j in range(CT):
                        i = V.match_replace(chosen[:, j * E:(j + 1) * E], top8[:, j, :],
                                            kept[:, j * E:(j + 1) * E], TAKEN)
                    step(i)
                    settled()
                    step(tt(chosen[:, :], chosen[:, :], kept[:, :], ALU.not_equal))
                elif part == 3:
                    settled()
                    step(tt(chosen[:, :], chosen[:, :], score[:, :], ALU.mult))
                    settled()
                    step(V.tensor_reduce(total[:, :], by_tile(chosen, E), AX_X, ALU.add))
                    settled()
                    step(V.tensor_scalar(total[:, :], total[:, :], 1e-20, None, ALU.add))
                elif part == 4:
                    settled()
                    step(V.reciprocal(inv[:, :], total[:, :]))
                    settled()
                    inv_b = inv[:, :].rearrange("p (t a) -> p t a", a=1).to_broadcast([P, CT, E])
                    step(tt(by_tile(chosen, E), by_tile(chosen, E), inv_b, ALU.mult))
                    settled()
                    step(V.tensor_scalar(chosen[:, :], chosen[:, :], SCALE, None, ALU.mult))
                else:
                    settled()
                    step(V.tensor_copy(mix[:, :, 0, :].bitcast(F32R), by_tile(chosen, E)))
                    settled()
                    step(tt(mix[:, :, 1, :], by_tile(chosen, E), mix[:, :, 0, :], ALU.subtract))

            def gated_product(c, p):
                dve.wait_ge(silu_done, SLOTS * c + p + 1)
                dve.wait_ge(up_done, SLOTS * c + p + 1)
                bank = mix_bank[1] if p == PAIRS else up_bank[p % 2]
                nc.vector.tensor_tensor(hid[:, p % 3, :], bank[:, :], hid[:, p % 3, :], ALU.mult).then_inc(gated, 1)

            def weighted_product(c, p):
                dve.wait_ge(gated, SLOTS * c + p + 1)
                dve.wait_ge(mix_done, PAIRS * c + p + 1)
                nc.vector.tensor_tensor(hid[:, p % 3, :], mix_bank[p % 2][:, :], hid[:, p % 3, :],
                                        ALU.mult).then_inc(weighted, 1)

            def update_x(c):
                dve.wait_ge(y_turned, c + 1)
                t = x_all[:, tiles(c), :].rearrange("p t d -> p (t d)")
                nc.vector.tensor_tensor(t, misc[:, :], t, ALU.add).then_inc(x_updated, 1)

            def slot(c, q, last):
                if q < SLOTS or not last:
                    n, p = place(c, q)
                    gated_product(n, p)
                    if p < PAIRS:
                        weighted_product(n, p)
                if not last and q >= LEAD_F:
                    if q == 6:
                        ln_moments(c + 1)
                    if q == 8:
                        ln_apply(c + 1)
                    if q == 10:
                        xT_low(c + 1)
                    if q in (15, 17, 19, 22, 24, 26):
                        route(c + 1, (15, 17, 19, 22, 24, 26).index(q))
                if q == SLOTS + 3:
                    update_x(c)

            ln_moments(0)
            ln_apply(0)
            xT_low(0)
            for part in range(6):
                route(0, part)
            run(dve, slot)

        @block.gpsimd
        def _(pool):
            def rstd_of(n):
                pool.wait_ge(ln_step, LN_STEPS * n + 2)
                nc.gpsimd.tensor_tensor(veps[:, :], moments[:, :, 1], w["eps"][:, 0:veps.shape[1]], ALU.add).then_inc(rstd_step, 1)
                pool.wait_ge(rstd_step, 2 * n + 1)
                if not (isinstance(n, int) and n == 0):
                    pool.wait_ge(ln_step, LN_STEPS * n)
                nc.gpsimd.tensor_tensor(rstd[:, :], veps[:, :], w["minus_half"][:, :], ALU.pow).then_inc(rstd_step, 1)

            def low(c, p):
                pool.wait_ge(hid_hi_done, SLOTS * c + p + 1)
                nc.gpsimd.tensor_tensor(hid_lo[:, p % 3, :], hid[:, p % 3, :],
                                        hid_hi[:, p % 3, :].bitcast(F32), ALU.subtract).then_inc(hid_lo_done, 1)

            def slot(c, q, last):
                if q < SLOTS or not last:
                    low(*place(c, q))
                if not last and q == 7:
                    rstd_of(c + 1)

            rstd_of(0)
            run(pool, slot)

        if out is not None:
            @block.sync
            def _(sp):
                with sp.Fori(0, NC) as c:
                    sp.wait_ge(x_updated, c + 1)
                    sp.dma_start(out[:, tiles(c), :], x_all[:, tiles(c), :]).then_inc(stored, 16)
                sp.wait_ge(stored, 16 * NC)


def attention(nc, w, x_all, psum):
    TB = SEQ // P
    NB = x_all.shape[1] // TB
    QUADS = H // 4
    STEPS = 2 * QUADS
    NPB = P + SEQ
    scores_late, scores_early = psum[0:2], psum[2]
    turn_bank = psum[3:5]
    o_bank, proj_bank, acc = psum[5], psum[6], psum[7]
    with ExitStack() as ctx:
        def sb(name, shape, dt=F32):
            return ctx.enter_context(nc.sbuf_tensor("a_" + name, shape, dt))

        def sem(name):
            return ctx.enter_context(nc.semaphore("a_" + name))

        xn = sb("xn", [P, TB, D])
        stats, moments = sb("stats", [P, TB, 6]), sb("moments", [P, TB, 2])
        veps, rstd = sb("veps", [P, TB]), sb("rstd", [P, TB])
        hold = sb("hold", [P, 1])
        xT_hi = sb("xT_hi", [P, 2, SEQ], F32R)
        xT_lo = sb("xT_lo", [P, 2, SEQ], F32R)
        qT = sb("qT", [P, 2, 2, SEQ])
        kZ = sb("kZ", [P, 2, 2, 2, SEQ])
        v = sb("v", [P, 2, TB, 4 * HD])
        prob = sb("prob", [P, 2, 4 * NPB])
        probT = sb("probT", [P, 4 * NPB])
        oT = sb("oT", [P, 2, 2, SEQ])
        yT = sb("yT", [P, SEQ])
        top, bias = sb("top", [P, 2, 2, 2, 2]), sb("bias", [P, 2, 2, 2, 2])
        mass, inv = sb("mass", [P, 2, 2, 2, 2]), sb("inv", [P, 2, 2, 2, 2])

        zeroed = sem("zeroed")
        ln_step, rstd_step, xn_turned = sem("ln_step"), sem("rstd_step"), sem("xn_turned")
        xT_hi_done, xT_lo_done = sem("xT_hi_done"), sem("xT_lo_done")
        proj_done, proj_read = sem("proj_done"), sem("proj_read")
        scores_done, top_step, bias_done = sem("scores_done"), sem("top_step"), sem("bias_done")
        exp_done, inv_done, normed = sem("exp_done"), sem("inv_done"), sem("normed")
        prob_turned, probT_done = sem("prob_turned"), sem("probT_done")
        o_done, oT_done, out_done = sem("o_done"), sem("oT_done"), sem("out_done")
        yT_done, y_turned, x_updated = sem("yT_done"), sem("y_turned"), sem("x_updated")

        LN_STEPS = 3

        def at(c, k):
            return STEPS * c + k, 2 * c + k // QUADS

        def tiles(b):
            return slice(b * TB, (b + 1) * TB) if isinstance(b, int) else bass.ds(b * TB, TB)

        def run(engine, engine_slot):
            for k in range(LEAD_A):
                engine_slot(0, k, False)
            with engine.Fori(0, NB // 2 - 1) as c:
                for k in range(LEAD_A, STEPS + LEAD_A):
                    engine_slot(c, k, False)
            for k in range(LEAD_A, STEPS + LEAD_A):
                engine_slot(NB // 2 - 1, k, True)

        block = ctx.enter_context(nc.Block())

        @block.tensor
        def _(pe):
            def turn_xn(c, k):
                s, b = at(c, k)
                pe.wait_ge(ln_step, LN_STEPS * (b + 1) + 3)
                if k < LEAD_A:
                    pe.wait_ge(proj_read, 3 * s + 3)
                else:
                    pe.wait_ge(x_updated, b)
                turn_xn_tiles()

            def turn_xn_tiles():
                for j in range(TB):
                    mm = nc.tensor.transpose(proj_bank[:, j * P:(j + 1) * P], xn[:, j, :], w["ident"][:, :])
                mm.then_inc(xn_turned, 1)

            def project(c, k, last):
                s, b = at(c, k)
                side, quad = k // QUADS % 2, k % QUADS
                xh, xl = xT_hi[:, side, :], xT_lo[:, side, :]
                if quad == 0:
                    pe.wait_ge(xT_lo_done, b + 1)
                if quad == 3:
                    if last and k == STEPS - 1:
                        pe.wait_ge(x_updated, b)
                    else:
                        pe.wait_ge(xT_lo_done, b + 2)
                for a, kind in enumerate(("pq", "pk")):
                    pe.wait_ge(proj_read, 3 * s + a)
                    for pair in range(2):
                        cols = slice((2 * quad + pair) * P, (2 * quad + pair + 1) * P)
                        o = proj_bank[:, pair * SEQ:(pair + 1) * SEQ]
                        hi, lo = w[kind + "_hi"][:, cols], w[kind + "_lo"][:, cols]
                        nc.tensor.matmul(o, hi, xh, start=True, stop=False)
                        nc.tensor.matmul(o, lo, xh, start=False, stop=False)
                        mm = nc.tensor.matmul(o, hi, xl, start=False, stop=True)
                    mm.then_inc(proj_done, 1)
                pe.wait_ge(proj_read, 3 * s + 2)
                cols = slice(quad * 4 * HD, (quad + 1) * 4 * HD)
                hi, lo = w["pv_hi"][:, cols], w["pv_lo"][:, cols]
                for j in range(TB):
                    o = proj_bank[:, j * SEQ:(j + 1) * SEQ]
                    t = slice(j * P, (j + 1) * P)
                    nc.tensor.matmul(o, xh[:, t], hi, start=True, stop=False)
                    nc.tensor.matmul(o, xh[:, t], lo, start=False, stop=False)
                    mm = nc.tensor.matmul(o, xl[:, t], hi, start=False, stop=True)
                mm.then_inc(proj_done, 1)

            def scores(c, k):
                s, _ = at(c, k)
                i = k % 2
                pe.wait_ge(proj_read, 3 * s + 2)
                pe.wait_ge(exp_done, 2 * s)
                for pair in range(2):
                    early = scores_early[:, pair * SEQ:(pair + 1) * SEQ]
                    nc.tensor.matmul(early, qT[:, i, pair, 0:P], kZ[:, i, pair, :, 0:P], start=True, stop=False)
                    nc.tensor.matmul(early, w["ident_b"][:, :], w["mask"][:, :], start=False, stop=True)
                for pair in range(2):
                    late = scores_late[pair]
                    nc.tensor.matmul(late[:, :], qT[:, i, pair, P:SEQ], kZ[:, i, pair, :, :], start=True, stop=False)
                    nc.tensor.matmul(late[:, :].rearrange("p (h n) -> p h n", h=2)[:, :, P:SEQ], w["ident_b"][:, :],
                                     w["mask"][:, :], start=False, stop=True).then_inc(scores_done, 1)

            def turn_prob(c, k):
                s, _ = at(c, k)
                for g in range(3):
                    pe.wait_ge(normed, 2 * s + (1 if g == 0 else 2))
                    if not (isinstance(c, int) and c == 0 and 3 * k + g < 2):
                        pe.wait_ge(probT_done, 3 * s + g - 1)
                    bank = turn_bank[(3 * k + g) % 2]
                    for j in range(4):
                        n = 4 * g + j
                        mm = nc.tensor.transpose(bank[:, j * P:(j + 1) * P], prob[:, k % 2, n * P:(n + 1) * P],
                                                 w["ident"][:, :])
                    mm.then_inc(prob_turned, 1)

            def weigh_values(c, k):
                s, _ = at(c, k)
                i = k % 2
                pe.wait_ge(proj_read, 3 * s + 3)
                pe.wait_ge(oT_done, s)
                for pair in range(2):
                    pe.wait_ge(probT_done, 3 * s + 2 + pair)
                    for kb in range(2):
                        for h in range(2):
                            hh = 2 * pair + h
                            cols = slice(hh * NPB + kb * SEQ, hh * NPB + (SEQ if kb == 0 else NPB))
                            mm = nc.tensor.matmul(o_bank[h * HD:(h + 1) * HD, pair * SEQ + kb * P:(pair + 1) * SEQ],
                                                  v[:, i, kb, hh * HD:(hh + 1) * HD], probT[:, cols],
                                                  start=(kb == 0), stop=(kb == 1))
                mm.then_inc(o_done, 1)

            def output(c, k):
                s, b = at(c, k)
                quad = k % QUADS
                pe.wait_ge(oT_done, s + 1)
                if quad == 0:
                    pe.wait_ge(yT_done, b)
                for pair in range(2):
                    n = 2 * quad + pair
                    mm = nc.tensor.matmul(acc[:, 0:SEQ], w["po"][:, n * P:(n + 1) * P],
                                          oT[:, k % 2, pair, :], start=(n == 0), stop=(n == 2 * QUADS - 1))
                mm.then_inc(out_done, 1)

            def turn_y(c, k, last):
                s, b = at(c, k)
                pe.wait_ge(yT_done, b)
                if k < STEPS or not last:
                    pe.wait_ge(proj_read, 3 * s + 3)
                for j in range(TB):
                    mm = nc.tensor.transpose(proj_bank[:, j * P:(j + 1) * P], yT[:, j * P:(j + 1) * P],
                                             w["ident"][:, :])
                mm.then_inc(y_turned, 1)

            def slot(c, k, last):
                first = k < LEAD_A
                live = k < STEPS or not last
                if live:
                    project(c, k, last)
                if k >= 2 and (k - 2 < STEPS or not last):
                    output(c, k - 2)
                if k % QUADS == 2 and not first:
                    turn_y(c, k, last)
                if k % QUADS == 2 and not last:
                    turn_xn(c, k)
                if k >= 1 and (k - 1 < STEPS or not last):
                    turn_prob(c, k - 1)
                    weigh_values(c, k - 1)
                if live:
                    scores(c, k)

            pe.wait_ge(ln_step, LN_STEPS)
            turn_xn_tiles()
            run(pe, slot)

        @block.scalar
        def _(act):
            def xT_high(n, side):
                act.wait_ge(xn_turned, n + 1)
                nc.scalar.copy(xT_hi[:, side, :], proj_bank[:, 0:SEQ]).then_inc(xT_hi_done, 1)

            def exps(c, k):
                s, _ = at(c, k)
                i = k % 2
                if not (isinstance(c, int) and c == 0 and k < 2):
                    act.wait_ge(prob_turned, 3 * s - 3)
                for pair in range(2):
                    act.wait_ge(bias_done, 2 * s + pair + 1)
                    early = scores_early[:, pair * SEQ:(pair + 1) * SEQ]
                    for h in range(2):
                        o = (2 * pair + h) * NPB
                        nc.scalar.activation(prob[:, i, o:o + P], early[:, h * P:(h + 1) * P], ACT.Exp,
                                             bias=bias[:, i, pair, 0, h:h + 1], scale=HD ** -0.5,
                                             accum_out=mass[:, i, pair, 0, h:h + 1])
                        e = nc.scalar.activation(prob[:, i, o + P:o + NPB],
                                                 scores_late[pair][:, h * SEQ:(h + 1) * SEQ], ACT.Exp,
                                                 bias=bias[:, i, pair, 1, h:h + 1], scale=HD ** -0.5,
                                                 accum_out=mass[:, i, pair, 1, h:h + 1])
                    e.then_inc(exp_done, 1)

            def copy_probT(c, k):
                s, _ = at(c, k)
                for g in range(3):
                    act.wait_ge(prob_turned, 3 * s + g + 1)
                    if g == 0:
                        act.wait_ge(o_done, s)
                    nc.scalar.copy(probT[:, g * 4 * P:(g + 1) * 4 * P],
                                   turn_bank[(3 * k + g) % 2][:, :]).then_inc(probT_done, 1)

            def copy_y(c, k):
                _, b = at(c, k)
                act.wait_ge(out_done, QUADS * b)
                nc.scalar.copy(yT[:, :], acc[:, 0:SEQ]).then_inc(yT_done, 1)

            def slot(c, k, last):
                if k % QUADS == 2 and k >= LEAD_A:
                    copy_y(c, k)
                if k >= 1 and (k - 1 < STEPS or not last):
                    exps(c, k - 1)
                    if k % QUADS == 2 and not last:
                        xT_high(at(c, k)[1] + 1, (k // QUADS + 1) % 2)
                    copy_probT(c, k - 1)
                elif k % QUADS == 2 and not last:
                    xT_high(at(c, k)[1] + 1, (k // QUADS + 1) % 2)

            xT_high(0, 0)
            run(act, slot)

        @block.vector
        def _(dve):
            def ln_moments(n):
                if not (isinstance(n, int) and n == 0):
                    dve.wait_ge(rstd_step, 2 * n)
                for j in range(TB):
                    i = nc.vector.bn_stats(stats[:, j, :], x_all[:, tiles(n), :][:, j, :])
                i.then_inc(ln_step, 1)
                dve.wait_ge(ln_step, LN_STEPS * n + 1)
                nc.vector.memset(hold[:, :], 0.0)
                for j in range(TB):
                    i = nc.vector.bn_aggr(moments[:, j, :], stats[:, j, :])
                i.then_inc(ln_step, 1)

            def ln_apply(n):
                dve.wait_ge(rstd_step, 2 * n + 2)
                dve.wait_ge(xn_turned, n)
                for j in range(TB):
                    i = nc.vector.tensor_scalar(xn[:, j, :], x_all[:, tiles(n), :][:, j, :], moments[:, j, 0:1],
                                                rstd[:, j:j + 1], ALU.subtract, ALU.mult)
                i.then_inc(ln_step, 1)

            def xT_low(n, side):
                dve.wait_ge(xT_hi_done, n + 1)
                nc.vector.tensor_tensor(xT_lo[:, side, :], proj_bank[:, 0:SEQ], xT_hi[:, side, :].bitcast(F32),
                                        ALU.subtract).then_inc(xT_lo_done, 1)

            def copy_qk(c, k):
                s, _ = at(c, k)
                i = k % 2
                if not (isinstance(c, int) and c == 0 and k < 2):
                    dve.wait_ge(scores_done, 2 * s - 2)
                dve.wait_ge(proj_done, 3 * s + 1)
                nc.vector.tensor_copy(qT[:, i, :, :], proj_bank[:, :].rearrange("p (a n) -> p a n", a=2))\
                    .then_inc(proj_read, 1)
                dve.wait_ge(proj_done, 3 * s + 2)
                for h in range(2):
                    rows = slice(h * HD, (h + 1) * HD)
                    cp = nc.vector.tensor_copy(kZ[rows, i, :, h, :],
                                               proj_bank[rows, :].rearrange("p (a n) -> p a n", a=2))
                cp.then_inc(proj_read, 1)

            def copy_v(c, k):
                s, _ = at(c, k)
                if not (isinstance(c, int) and c == 0 and k < 2):
                    dve.wait_ge(o_done, s - 1)
                dve.wait_ge(proj_done, 3 * s + 3)
                nc.vector.tensor_copy(v[:, k % 2, :, :], proj_bank[:, :].rearrange("p (a n) -> p a n", a=TB))\
                    .then_inc(proj_read, 1)

            def normalise(c, k, pair):
                s, _ = at(c, k)
                i = k % 2
                dve.wait_ge(exp_done, 2 * s + pair + 1)
                nc.vector.reciprocal(inv[:, i, pair, :, :], mass[:, i, pair, :, :]).then_inc(inv_done, 1)
                dve.wait_ge(inv_done, 2 * s + pair + 1)
                for h in range(2):
                    o = (2 * pair + h) * NPB
                    for late, (a, b) in enumerate(((o, o + P), (o + P, o + NPB))):
                        m = nc.vector.tensor_scalar(prob[:, i, a:b], prob[:, i, a:b],
                                                    inv[:, i, pair, late, h:h + 1], None, ALU.mult)
                m.then_inc(normed, 1)

            def copy_o(c, k):
                s, _ = at(c, k)
                if not (isinstance(c, int) and c == 0 and k < 2):
                    dve.wait_ge(out_done, s - 1)
                dve.wait_ge(o_done, s + 1)
                nc.vector.tensor_copy(oT[:, k % 2, :, :], o_bank[:, :].rearrange("p (a n) -> p a n", a=2))\
                    .then_inc(oT_done, 1)

            def maxima(c, k):
                s, _ = at(c, k)
                i = k % 2
                for pair in range(2):
                    dve.wait_ge(scores_done, 2 * s + pair + 1)
                    if pair == 0:
                        early = scores_early[:, :].rearrange("p (a h n) -> p a h n", a=2, h=2)
                        nc.vector.tensor_reduce(top[:, i, :, 0, :], early, AX_X, ALU.max)
                    late = scores_late[pair][:, :].rearrange("p (h n) -> p h n", h=2)
                    nc.vector.tensor_reduce(top[:, i, pair, 1, :], late, AX_X, ALU.max).then_inc(top_step, 1)
                    dve.wait_ge(top_step, 2 * s + pair + 1)
                    nc.vector.tensor_scalar(bias[:, i, pair, :, :], top[:, i, pair, :, :], -HD ** -0.5, None,
                                            ALU.mult).then_inc(bias_done, 1)

            def update_x(c, k):
                _, b = at(c, k)
                dve.wait_ge(y_turned, b)
                t = x_all[:, tiles(b - 1), :].rearrange("p t d -> p (t d)")
                nc.vector.tensor_tensor(t, proj_bank[:, 0:SEQ], t, ALU.add).then_inc(x_updated, 1)

            def slot(c, k, last):
                live = k < STEPS or not last
                soft = k >= 1 and (k - 1 < STEPS or not last)
                b = at(c, k)[1]
                if k % QUADS == 1 and not last:
                    ln_moments(b + 1)
                if live:
                    copy_qk(c, k)
                if soft:
                    normalise(c, k - 1, 0)
                if live:
                    copy_v(c, k)
                if soft:
                    normalise(c, k - 1, 1)
                if k % QUADS == 1 and not last:
                    ln_apply(b + 1)
                if k % QUADS == 2 and k >= LEAD_A:
                    update_x(c, k)
                if k % QUADS == 2 and not last:
                    xT_low(b + 1, (k // QUADS + 1) % 2)
                if soft:
                    copy_o(c, k - 1)
                if live:
                    maxima(c, k)

            for i in range(2):
                for h in range(2):
                    rows = slice((1 - h) * HD, (2 - h) * HD)
                    nc.vector.memset(kZ[rows, i, :, h, :], 0.0)
            ln_moments(0)
            ln_apply(0)
            xT_low(0, 0)
            run(dve, slot)

        @block.gpsimd
        def _(pool):
            def rstd_of(n):
                pool.wait_ge(ln_step, LN_STEPS * n + 2)
                nc.gpsimd.tensor_tensor(veps[:, :], moments[:, :, 1], w["eps"][:, 0:veps.shape[1]], ALU.add).then_inc(rstd_step, 1)
                pool.wait_ge(rstd_step, 2 * n + 1)
                nc.gpsimd.tensor_tensor(rstd[:, :], veps[:, :], w["minus_half"][:, 0:TB], ALU.pow)\
                    .then_inc(rstd_step, 1)

            rstd_of(0)
            with pool.Fori(1, NB) as n:
                rstd_of(n)


def macaron(nc, x, P_q, P_k, P_v, P_o, gate_w, gate_bias, We_gate, We_up, We_down, Ws_gate, Ws_up, Ws_down, out):
    B, M, _ = x.shape
    tiles = B * M // P
    dr = {"pq": P_q, "pk": P_k, "pv": P_v, "po": P_o, "gw": gate_w, "wg": We_gate, "wu": We_up, "wd": We_down,
          "sg": Ws_gate, "su": Ws_up, "sd": Ws_down,
          "gb": gate_bias.rearrange("(a e) -> a e", a=1).to_broadcast([P, E])}
    x_v = x.rearrange("b (t p) d -> p (b t) d", p=P)
    out_v = out.rearrange("b (t p) d -> p (b t) d", p=P)
    with ExitStack() as ctx:
        def sb(name, shape, dt=F32):
            return ctx.enter_context(nc.sbuf_tensor(name, shape, dt))

        x_all = sb("x_all", [P, tiles, D])
        w = {}
        for kind in ("wg", "wu", "wd"):
            for part in ("_hi", "_lo"):
                w[kind + part] = sb(kind + part, [P, SLOTS * P], F32R)
        for kind in ("pq", "pk", "pv"):
            for part in ("_hi", "_lo"):
                w[kind + part] = sb(kind + part, [P, H * HD], F32R)
        w["po"] = sb("po", [P, H * HD])
        w["gw_hi"], w["gw_lo"] = sb("gw_hi", [P, P], F32R), sb("gw_lo", [P, P], F32R)
        w["sel"] = sb("sel", [P, PAIRS * P], F32R)
        w["bias"] = sb("gate_bias", [P, E])
        w["ident"] = sb("ident", [P, P])
        w["ident_b"] = sb("ident_b", [P, P], BF16)
        w["mask"] = sb("mask", [P, 2 * P], BF16)
        w["earlier"] = sb("earlier", [P, E])
        w["minus_half"] = sb("minus_half", [P, CT])
        w["eps"] = sb("eps", [P, CT])
        psum = [ctx.enter_context(nc.psum_tensor(f"bank{i}", [P, 512], F32)) for i in range(8)]

        setup(nc, w, x_v, x_all, dr, psum)
        ffn(nc, "f1_", w, x_all, psum, None)
        attention(nc, w, x_all, psum)
        ffn(nc, "f2_", w, x_all, psum, out_v)


_INS = ["L0_attn_x", "L0_attn_P_q", "L0_attn_P_k", "L0_attn_P_v", "L0_attn_P_o", "L0_ffn_gate_w", "L0_ffn_gate_bias",
        "L0_ffn_We_gate", "L0_ffn_We_up", "L0_ffn_We_down", "L0_ffn_Ws_gate", "L0_ffn_Ws_up", "L0_ffn_Ws_down"]


def kernel(**inputs):
    import numpy as _np
    import concourse.bacc as _bacc
    from concourse import mybir as _mybir
    from concourse.bass_utils import run_bass_kernel_spmd as _run

    nc = _bacc.Bacc("TRN2", target_bir_lowering=False, num_devices=1)
    arrays, args = {}, []
    for name in _INS:
        a = _np.ascontiguousarray(inputs[name])
        arrays[f"in_{name}"] = a
        args.append(nc.dram_tensor(f"in_{name}", a.shape, _mybir.dt.from_np(a.dtype), kind="ExternalInput").ap())
    x = arrays["in_L0_attn_x"]
    out = nc.dram_tensor("out_0", x.shape, _mybir.dt.from_np(x.dtype), kind="ExternalOutput").ap()
    macaron(nc, *args, out)
    r = _run(nc, [arrays], core_ids=[0])
    return r.results[0]["out_0"]
```

```python
from contextlib import ExitStack

import concourse.bass as bass
from concourse import mybir

F32 = mybir.dt.float32
F32R = mybir.dt.float32r
BF16 = mybir.dt.bfloat16
ALU = mybir.AluOpType
ACT = mybir.ActivationFunctionType
AX_X = mybir.AxisListType.X

P = 128
D = 128
E = 64
F = 64
NG = 8
TOPK_GROUPS = 4
PAIRS = E // 2
SLOTS = PAIRS + 1
H = 16
HD = 64
SEQ = 256
CT = 4
CHUNK = CT * P
SCALE = 2.5
LN_EPS = 1e-5
OFF = -3.0e38
TAKEN = -3.3e38
MASKED = -1.0e30
LEAD_F = 6
LEAD_A = 3


def setup(nc, w, x, x_all, dr, psum):
    SW = 1024
    with ExitStack() as ctx:
        def sb(name, shape, dt=F32):
            return ctx.enter_context(nc.sbuf_tensor(name, shape, dt))

        def sem(name):
            return ctx.enter_context(nc.semaphore(name))

        NST = 6
        stage = sb("stage", [P, NST, SW])
        po_raw = sb("po_raw", [P, H * HD])
        gw_raw = sb("gw_raw", [E, D])
        sel_raw = sb("sel_raw", [P, SW])
        mask_raw = sb("mask_raw", [P, 2, P])
        landed = [sem(f"landed{i}") for i in range(NST)]
        x_landed, small_landed = sem("x_landed"), sem("small_landed")
        hi_split, lo_split = sem("hi_split"), sem("lo_split")
        const_step, ident_ready = sem("const_step"), sem("ident_ready")
        sel_step, sel_copied = sem("sel_step"), sem("sel_copied")
        turned, turned_copied, gw_hi = sem("turned"), sem("turned_copied"), sem("gw_hi")

        pieces = []
        for j in range(4):
            n = SW // F
            for kind in ("wg", "wu"):
                c = slice(j * SW, (j + 1) * SW)
                pieces.append((w[kind + "_hi"][:, c], w[kind + "_lo"][:, c],
                               dr[kind][j * n:(j + 1) * n].rearrange("e d f -> d e f"), (P, n, F)))
            n = SW // D
            c = slice(j * SW, (j + 1) * SW)
            pieces.append((w["wd_hi"][:, c], w["wd_lo"][:, c],
                           dr["wd"][2 * j * n:2 * (j + 1) * n].rearrange("(n t) f h -> (t f) n h", t=2), (P, n, D)))
        for kind, src in (("wg", "sg"), ("wu", "su")):
            c = slice(PAIRS * P, PAIRS * P + F)
            pieces.append((w[kind + "_hi"][:, c], w[kind + "_lo"][:, c], dr[src], (P, F)))
        c = slice(PAIRS * P, PAIRS * P + D)
        pieces.append((w["wd_hi"][0:F, c], w["wd_lo"][0:F, c], dr["sd"], (F, D)))
        for kind in ("pq", "pk", "pv"):
            pieces.append((w[kind + "_hi"][:, :], w[kind + "_lo"][:, :],
                           dr[kind].rearrange("h d k -> d h k"), (P, H, HD)))

        def staged(n):
            shape = pieces[n][3]
            cols = shape[1] * (shape[2] if len(shape) == 3 else 1)
            return stage[0:shape[0], n % NST, 0:cols]

        block = ctx.enter_context(nc.Block())

        @block.sync
        def _(sp):
            for n, (_, _, src, shape) in enumerate(pieces):
                if n >= NST:
                    sp.wait_ge(lo_split, n - NST + 1)
                dst = staged(n)
                if len(shape) == 3:
                    dst = dst.rearrange("p (a b) -> p a b", b=shape[2])
                sp.dma_start(dst, src).then_inc(landed[n % NST], 16)

        @block.gpsimd
        def _(pool):
            nc.gpsimd.memset(w["ident"][:, :], 0.0).then_inc(const_step, 1)
            nc.gpsimd.memset(mask_raw[:, :, :], 0.0).then_inc(const_step, 1)
            pool.wait_ge(const_step, 2)
            nc.gpsimd.affine_select(out=w["ident"][:, :], in_=w["ident"][:, :], compare_op=ALU.not_equal,
                                    fill=1.0, base=0, pattern=[[-1, P]], channel_multiplier=1).then_inc(ident_ready, 1)
            nc.gpsimd.affine_select(out=mask_raw[:, :, :], in_=mask_raw[:, :, :], compare_op=ALU.is_ge,
                                    fill=MASKED, base=0, pattern=[[0, 2], [-1, P]],
                                    channel_multiplier=1).then_inc(ident_ready, 1)
            nc.gpsimd.memset(w["earlier"][:, :], 1.0).then_inc(const_step, 1)
            pool.wait_ge(const_step, 3)
            earlier = w["earlier"][:, :].rearrange("p (g h) -> p g h", h=NG)
            nc.gpsimd.affine_select(out=earlier, in_=earlier, compare_op=ALU.is_gt, fill=0.0, base=0,
                                    pattern=[[1, NG], [-1, NG]], channel_multiplier=0).then_inc(const_step, 1)
            nc.gpsimd.memset(w["minus_half"][:, :], -0.5).then_inc(const_step, 1)
            nc.gpsimd.memset(w["eps"][:, :], LN_EPS).then_inc(const_step, 1)
            for kind in ("gw_hi", "gw_lo"):
                nc.gpsimd.memset(w[kind][:, E:P].bitcast(F32), 0.0).then_inc(const_step, 1)
            for kind in ("wg_hi", "wg_lo", "wu_hi", "wu_lo"):
                nc.gpsimd.memset(w[kind][:, PAIRS * P + F:SLOTS * P].bitcast(F32), 0.0).then_inc(const_step, 1)
            for j in range(4):
                n = SW // P
                v = sel_raw[:, :].rearrange("p (n t c) -> p n t c", t=2, c=F)
                if j >= 1:
                    pool.wait_ge(sel_copied, j)
                nc.gpsimd.memset(sel_raw[:, :], 0.0).then_inc(sel_step, 1)
                for half in range(2):
                    pool.wait_ge(sel_step, 3 * j + half + 1)
                    nc.gpsimd.affine_select(out=v, in_=v, compare_op=ALU.not_equal, fill=1.0,
                                            base=-(half * E + 2 * j * n), pattern=[[-2, n], [-1, 2], [0, F]],
                                            channel_multiplier=1).then_inc(sel_step, 1)

        @block.scalar
        def _(act):
            act.dma_start(x_all[:, 0:CT, :], x[:, 0:CT, :]).then_inc(x_landed, 16)
            act.dma_start(gw_raw[:, :], dr["gw"]).then_inc(small_landed, 16)
            act.dma_start(w["bias"][:, :], dr["gb"]).then_inc(small_landed, 16)
            act.dma_start(po_raw[:, :].rearrange("d (h v) -> d h v", v=HD),
                          dr["po"].rearrange("h d v -> d h v")).then_inc(small_landed, 16)
            act.dma_start(x_all[:, CT:, :], x[:, CT:, :]).then_inc(x_landed, 16)
            act.wait_ge(ident_ready, 2)
            nc.scalar.copy(w["mask"][:, :], mask_raw[:, :, :].rearrange("p a b -> p (a b)"))
            nc.scalar.copy(w["ident_b"][:, :], w["ident"][:, :])
            act.wait_ge(turned, 1)
            nc.scalar.copy(w["gw_hi"][:, 0:E], psum[2][:, 0:E]).then_inc(gw_hi, 1)
            for j in range(4):
                act.wait_ge(sel_step, 3 * j + 3)
                nc.scalar.copy(w["sel"][:, j * SW:(j + 1) * SW], sel_raw[:, :]).then_inc(sel_copied, 1)
            for n, (hi, _, _, _) in enumerate(pieces):
                act.wait_ge(landed[n % NST], 16 * (n // NST + 1))
                nc.scalar.copy(hi, staged(n)).then_inc(hi_split, 1)
            act.wait_ge(x_landed, 32)

        @block.vector
        def _(dve):
            for kind in ("wd_hi", "wd_lo"):
                nc.vector.memset(w[kind][F:P, PAIRS * P:SLOTS * P].bitcast(F32), 0.0)
            dve.wait_ge(gw_hi, 1)
            nc.vector.tensor_tensor(w["gw_lo"][:, 0:E], psum[2][:, 0:E], w["gw_hi"][:, 0:E].bitcast(F32),
                                    ALU.subtract)
            for b in range(2):
                dve.wait_ge(turned, b + 2)
                nc.vector.tensor_copy(w["po"][:, 4 * b * P:4 * (b + 1) * P], psum[b][:, :])
            for n, (hi, lo, _, _) in enumerate(pieces):
                dve.wait_ge(hi_split, n + 1)
                nc.vector.tensor_tensor(lo, staged(n), hi.bitcast(F32), ALU.subtract).then_inc(lo_split, 1)

        @block.tensor
        def _(pe):
            pe.wait_ge(ident_ready, 1)
            pe.wait_ge(small_landed, 48)
            nc.tensor.transpose(psum[2][:, 0:E], gw_raw[:, :], w["ident"][0:E, 0:E]).then_inc(turned, 1)
            for b in range(2):
                for j in range(4):
                    mm = nc.tensor.transpose(psum[b][:, j * P:(j + 1) * P],
                                             po_raw[:, (4 * b + j) * P:(4 * b + j + 1) * P], w["ident"][:, :])
                mm.then_inc(turned, 1)


def ffn(nc, tag, w, x_all, psum, out):
    NC = x_all.shape[1] // CT
    gate_bank, up_bank, mix_bank = psum[0:2], psum[2:4], psum[4:6]
    acc, misc = psum[6], psum[7]
    with ExitStack() as ctx:
        def sb(name, shape, dt=F32):
            return ctx.enter_context(nc.sbuf_tensor(tag + name, shape, dt))

        def sem(name):
            return ctx.enter_context(nc.semaphore(tag + name))

        xn = sb("xn", [P, CT, D])
        stats = sb("stats", [P, CT, 6])
        moments = sb("moments", [P, CT, 2])
        veps = sb("veps", [P, CT])
        rstd = sb("rstd", [P, CT])
        hold = sb("hold", [P, 1])
        xT_hi = sb("xT_hi", [P, 2 * CHUNK], F32R)
        xT_lo = sb("xT_lo", [P, 2 * CHUNK], F32R)
        mixT = sb("mixT", [P, 2 * CHUNK], F32R)
        hid = sb("hid", [P, 3, CHUNK])
        hid_hi = sb("hid_hi", [P, 3, CHUNK], F32R)
        hid_lo = sb("hid_lo", [P, 3, CHUNK], F32R)
        yT = sb("yT", [P, CHUNK])
        score = sb("score", [P, CT * E])
        biased = sb("biased", [P, CT * E])
        kept = sb("kept", [P, CT * E])
        chosen = sb("chosen", [P, CT * E])
        mix = sb("mix", [P, CT, 2, E])
        h4, l4 = sb("h4", [P, CT * NG, 4]), sb("l4", [P, CT * NG, 4])
        h2, m2, l2 = (sb(n, [P, CT * NG, 2]) for n in ("h2", "m2", "l2"))
        h1, m1, l1 = (sb(n, [P, CT * NG]) for n in ("h1", "m1", "l1"))
        gscore, rank, keep, drop = (sb(n, [P, CT * NG]) for n in ("gscore", "rank", "keep", "drop"))
        top8 = sb("top8", [P, CT, 8])
        total, inv = sb("total", [P, CT]), sb("inv", [P, CT])

        gate_done, up_done, mix_done, down_done = sem("gate_done"), sem("up_done"), sem("mix_done"), sem("down_done")
        silu_done, gated, weighted = sem("silu_done"), sem("gated"), sem("weighted")
        hid_hi_done, hid_lo_done = sem("hid_hi_done"), sem("hid_lo_done")
        yT_done, y_turned, x_updated = sem("yT_done"), sem("y_turned"), sem("x_updated")
        ln_step, rstd_step, xn_turned = sem("ln_step"), sem("rstd_step"), sem("xn_turned")
        xT_hi_done, xT_lo_done = sem("xT_hi_done"), sem("xT_lo_done")
        logits_done, score_done, route_step = sem("logits_done"), sem("score_done"), sem("route_step")
        mix_turned, mixT_done, stored = sem("mix_turned"), sem("mixT_done"), sem("stored")

        LN_STEPS = 3
        ROUTE_STEPS = 27
        ROUTE_FROM = 16

        def place(c, q):
            return (c, q) if q < SLOTS else (c + 1, q - SLOTS)

        def tiles(c):
            return slice(c * CT, (c + 1) * CT) if isinstance(c, int) else bass.ds(c * CT, CT)

        def half(c, width):
            o = (c % 2) * width
            return slice(o, o + width) if isinstance(c, int) else bass.ds(o, width)

        def body(engine_slot, c, last):
            for q in range(LEAD_F, SLOTS + LEAD_F):
                if not last or q < SLOTS + 5:
                    engine_slot(c, q, last)

        def run(engine, engine_slot):
            for q in range(LEAD_F):
                engine_slot(0, q, False)
            with engine.Fori(0, NC - 1) as c:
                body(engine_slot, c, False)
            body(engine_slot, NC - 1, True)

        block = ctx.enter_context(nc.Block())

        @block.tensor
        def _(pe):
            def turn_xn(n):
                pe.wait_ge(ln_step, LN_STEPS * n + 3)
                for j in range(CT):
                    mm = nc.tensor.transpose(misc[:, j * P:(j + 1) * P], xn[:, j, :], w["ident"][:, :])
                mm.then_inc(xn_turned, 1)

            def logits(n):
                pe.wait_ge(xT_lo_done, n + 1)
                for a, (wk, xt) in enumerate((("gw_hi", xT_hi), ("gw_lo", xT_hi), ("gw_hi", xT_lo))):
                    mm = nc.tensor.matmul(misc[:, :], w[wk][:, :], xt[:, half(n, CHUNK)],
                                          start=(a == 0), stop=(a == 2))
                mm.then_inc(logits_done, 1)

            def turn_logits(n):
                pe.wait_ge(score_done, 2 * n + 1)
                for j in range(CT):
                    mm = nc.tensor.transpose(misc[:, j * P:(j + 1) * P], yT[:, j * P:(j + 1) * P], w["ident"][:, :])
                mm.then_inc(logits_done, 1)

            def turn_mix(n):
                pe.wait_ge(route_step, ROUTE_STEPS * (n + 1))
                pe.wait_ge(score_done, 2 * n + 2)
                for j in range(CT):
                    mm = nc.tensor.transpose(misc[:, j * P:(j + 1) * P],
                                             mix[:, j, :, :].rearrange("p a b -> p (a b)"), w["ident"][:, :])
                mm.then_inc(mix_turned, 1)

            def three(bank, kind, p, rhs_hi, rhs_lo, start=True, stop=True):
                hi, lo = w[kind + "_hi"][:, p * P:(p + 1) * P], w[kind + "_lo"][:, p * P:(p + 1) * P]
                nc.tensor.matmul(bank[:, :], hi, rhs_hi, start=start, stop=False)
                nc.tensor.matmul(bank[:, :], lo, rhs_hi, start=False, stop=False)
                return nc.tensor.matmul(bank[:, :], hi, rhs_lo, start=False, stop=stop)

            def up(c, p):
                first = isinstance(c, int) and c == 0
                xh, xl = xT_hi[:, half(c, CHUNK)], xT_lo[:, half(c, CHUNK)]
                if p == 0:
                    pe.wait_ge(xT_lo_done, c + 1)
                if p == PAIRS:
                    g, u = mix_bank
                    pe.wait_ge(weighted, PAIRS * c + PAIRS - 1)
                else:
                    g, u = gate_bank[p % 2], up_bank[p % 2]
                    if p >= 2:
                        pe.wait_ge(silu_done, SLOTS * c + p - 1)
                    elif not first:
                        pe.wait_ge(silu_done, SLOTS * c + p - 2)
                three(g, "wg", p, xh, xl).then_inc(gate_done, 1)
                if p == PAIRS:
                    pe.wait_ge(weighted, PAIRS * c + PAIRS)
                elif p >= 2:
                    pe.wait_ge(gated, SLOTS * c + p - 1)
                elif not first:
                    pe.wait_ge(gated, SLOTS * c + p - 2)
                three(u, "wu", p, xh, xl).then_inc(up_done, 1)
                if p == PAIRS:
                    return
                if p == 0:
                    pe.wait_ge(mixT_done, c + 1)
                if p >= 2:
                    pe.wait_ge(weighted, PAIRS * c + p - 1)
                elif not first:
                    pe.wait_ge((silu_done, gated)[p], SLOTS * c)
                nc.tensor.matmul(mix_bank[p % 2][:, :], w["sel"][:, p * P:(p + 1) * P], mixT[:, half(c, CHUNK)],
                                 start=True, stop=True).then_inc(mix_done, 1)

            def down(c, p):
                pe.wait_ge(hid_lo_done, SLOTS * c + p + 1)
                if p == 0 and not (isinstance(c, int) and c == 0):
                    pe.wait_ge(yT_done, c)
                three(acc, "wd", p, hid_hi[:, p % 3, :], hid_lo[:, p % 3, :],
                      start=(p == 0), stop=(p == PAIRS)).then_inc(down_done, 1)

            def turn_y(c, last):
                pe.wait_ge(yT_done, c + 1)
                pe.wait_ge(mixT_done, c + 1 if last else c + 2)
                for j in range(CT):
                    mm = nc.tensor.transpose(misc[:, j * P:(j + 1) * P], yT[:, j * P:(j + 1) * P], w["ident"][:, :])
                mm.then_inc(y_turned, 1)

            def slot(c, q, last):
                if q < SLOTS or not last:
                    up(*place(c, q))
                if 3 <= q < SLOTS + 3 or (q >= SLOTS + 3 and not last):
                    down(*place(c, q - 3))
                if not last and q >= LEAD_F:
                    if q == 10:
                        turn_xn(c + 1)
                    if q == 12:
                        logits(c + 1)
                    if q == 14:
                        turn_logits(c + 1)
                    if q == 31:
                        turn_mix(c + 1)
                if q == SLOTS + 4:
                    turn_y(c, last)

            turn_xn(0)
            logits(0)
            turn_logits(0)
            turn_mix(0)
            run(pe, slot)

        @block.scalar
        def _(act):
            def xT_high(n):
                act.wait_ge(xn_turned, n + 1)
                nc.scalar.copy(xT_hi[:, half(n, CHUNK)], misc[:, :]).then_inc(xT_hi_done, 1)

            def sigmoid(n):
                act.wait_ge(logits_done, 2 * n + 1)
                nc.scalar.activation(yT[:, :], misc[:, :], ACT.Sigmoid).then_inc(score_done, 1)

            def copy_score(n):
                act.wait_ge(logits_done, 2 * n + 2)
                if not (isinstance(n, int) and n == 0):
                    act.wait_ge(route_step, ROUTE_STEPS * n)
                nc.scalar.copy(score[:, :].rearrange("p (t e) -> p t e", e=E),
                               misc[:, :].rearrange("p (t n) -> p t n", n=P)[:, :, 0:E]).then_inc(score_done, 1)

            def copy_mixT(n):
                act.wait_ge(mix_turned, n + 1)
                nc.scalar.copy(mixT[:, half(n, CHUNK)], misc[:, :]).then_inc(mixT_done, 1)

            def silu(c, p):
                act.wait_ge(gate_done, SLOTS * c + p + 1)
                if p >= 3 or not (isinstance(c, int) and c == 0):
                    act.wait_ge(hid_lo_done, SLOTS * c + p - 2)
                bank = mix_bank[0] if p == PAIRS else gate_bank[p % 2]
                nc.scalar.activation(hid[:, p % 3, :], bank[:, :], ACT.Silu).then_inc(silu_done, 1)

            def high(c, p):
                if p == PAIRS:
                    act.wait_ge(gated, SLOTS * (c + 1))
                else:
                    act.wait_ge(weighted, PAIRS * c + p + 1)
                if p >= 3 or not (isinstance(c, int) and c == 0):
                    act.wait_ge(down_done, SLOTS * c + p - 2)
                nc.scalar.copy(hid_hi[:, p % 3, :], hid[:, p % 3, :]).then_inc(hid_hi_done, 1)

            def copy_y(c):
                act.wait_ge(down_done, SLOTS * (c + 1))
                nc.scalar.mul(yT[:, :], acc[:, :], 0.5).then_inc(yT_done, 1)

            def slot(c, q, last):
                if q == SLOTS + 3:
                    copy_y(c)
                if q < SLOTS or not last:
                    silu(*place(c, q))
                if 1 <= q < SLOTS + 1 or (q >= SLOTS + 1 and not last):
                    high(*place(c, q - 1))
                if not last and q >= LEAD_F:
                    if q == 10:
                        xT_high(c + 1)
                    if q == 12:
                        sigmoid(c + 1)
                    if q == 14:
                        copy_score(c + 1)
                    if q == 31:
                        copy_mixT(c + 1)

            xT_high(0)
            sigmoid(0)
            copy_score(0)
            copy_mixT(0)
            run(act, slot)

        @block.vector
        def _(dve):
            def v8(t):
                return t[:, :].rearrange("p (g e) -> p g e", e=E // NG)

            def by_tile(t, n):
                return t[:, :].rearrange("p (t n) -> p t n", n=n)

            def by_group(t):
                return t[:, :].rearrange("p (g a) -> p g a", a=1).to_broadcast([P, CT * NG, E // NG])

            def ln_moments(n):
                if not (isinstance(n, int) and n == 0):
                    dve.wait_ge(rstd_step, 2 * n)
                for j in range(CT):
                    i = nc.vector.bn_stats(stats[:, j, :], x_all[:, tiles(n), :][:, j, :])
                i.then_inc(ln_step, 1)
                dve.wait_ge(ln_step, LN_STEPS * n + 1)
                nc.vector.memset(hold[:, :], 0.0)
                for j in range(CT):
                    i = nc.vector.bn_aggr(moments[:, j, :], stats[:, j, :])
                i.then_inc(ln_step, 1)

            def ln_apply(n):
                dve.wait_ge(rstd_step, 2 * n + 2)
                dve.wait_ge(xn_turned, n)
                for j in range(CT):
                    i = nc.vector.tensor_scalar(xn[:, j, :], x_all[:, tiles(n), :][:, j, :], moments[:, j, 0:1],
                                                rstd[:, j:j + 1], ALU.subtract, ALU.mult)
                i.then_inc(ln_step, 1)

            def xT_low(n):
                dve.wait_ge(xT_hi_done, n + 1)
                nc.vector.tensor_tensor(xT_lo[:, half(n, CHUNK)], misc[:, :],
                                        xT_hi[:, half(n, CHUNK)].bitcast(F32), ALU.subtract).then_inc(xT_lo_done, 1)

            def route(n, i):
                tt, V = nc.vector.tensor_tensor, nc.vector
                g8 = [P, CT, NG, NG]
                gs = by_tile(gscore, NG)
                best, ties = by_tile(kept, E), by_tile(chosen, E)
                if i == 0:
                    dve.wait_ge(score_done, 2 * n + 2)
                    dve.wait_ge(mix_turned, n)
                else:
                    dve.wait_ge(route_step, ROUTE_STEPS * n + i)
                if i == 0:
                    ins = tt(by_tile(biased, E), by_tile(score, E),
                             w["bias"][:, :].rearrange("p (a e) -> p a e", a=1).to_broadcast([P, CT, E]), ALU.add)
                elif i == 1:
                    tt(h4[:, :, :], v8(biased)[:, :, 0:4], v8(biased)[:, :, 4:8], ALU.max)
                    ins = tt(l4[:, :, :], v8(biased)[:, :, 0:4], v8(biased)[:, :, 4:8], ALU.min)
                elif i == 2:
                    tt(h2[:, :, :], h4[:, :, 0:2], h4[:, :, 2:4], ALU.max)
                    tt(m2[:, :, :], h4[:, :, 0:2], h4[:, :, 2:4], ALU.min)
                    ins = tt(l2[:, :, :], l4[:, :, 0:2], l4[:, :, 2:4], ALU.max)
                elif i == 3:
                    tt(h1[:, :], h2[:, :, 0], h2[:, :, 1], ALU.max)
                    tt(m1[:, :], h2[:, :, 0], h2[:, :, 1], ALU.min)
                    ins = tt(l2[:, :, :], l2[:, :, :], m2[:, :, :], ALU.max)
                elif i == 4:
                    ins = tt(l1[:, :], l2[:, :, 0], l2[:, :, 1], ALU.max)
                elif i == 5:
                    ins = tt(l1[:, :], l1[:, :], m1[:, :], ALU.max)
                elif i == 6:
                    ins = tt(gscore[:, :], h1[:, :], l1[:, :], ALU.add)
                elif i == 7:
                    ins = tt(best.rearrange("p t (g h) -> p t g h", g=NG),
                             gs.rearrange("p t (a g) -> p t a g", a=1).to_broadcast(g8),
                             gs.rearrange("p t (g a) -> p t g a", a=1).to_broadcast(g8), ALU.is_gt)
                elif i == 8:
                    ins = tt(ties.rearrange("p t (g h) -> p t g h", g=NG),
                             gs.rearrange("p t (a g) -> p t a g", a=1).to_broadcast(g8),
                             gs.rearrange("p t (g a) -> p t g a", a=1).to_broadcast(g8), ALU.is_equal)
                elif i == 9:
                    ins = tt(ties, ties, w["earlier"][:, :].rearrange("p (a e) -> p a e", a=1).to_broadcast([P, CT, E]),
                             ALU.mult)
                elif i == 10:
                    ins = tt(kept[:, :], kept[:, :], chosen[:, :], ALU.add)
                elif i == 11:
                    ins = V.tensor_reduce(rank[:, :], v8(kept), AX_X, ALU.add)
                elif i == 12:
                    ins = V.tensor_scalar(keep[:, :], rank[:, :], float(TOPK_GROUPS), None, ALU.is_lt)
                elif i == 13:
                    ins = V.tensor_scalar(drop[:, :], keep[:, :], -OFF, OFF, ALU.mult, ALU.add)
                elif i == 14:
                    ins = tt(v8(kept), v8(biased), by_group(keep), ALU.mult)
                elif i == 15:
                    ins = tt(v8(kept), v8(kept), by_group(drop), ALU.add)
                elif i == 16:
                    V.memset(hold[:, :], 0.0)
                    for j in range(CT):
                        ins = V.max(top8[:, j, :], kept[:, j * E:(j + 1) * E])
                elif i == 17:
                    V.memset(hold[:, :], 0.0)
                    for j in range(CT):
                        ins = V.match_replace(chosen[:, j * E:(j + 1) * E], top8[:, j, :],
                                              kept[:, j * E:(j + 1) * E], TAKEN)
                elif i == 18:
                    ins = tt(chosen[:, :], chosen[:, :], kept[:, :], ALU.not_equal)
                elif i == 19:
                    ins = tt(chosen[:, :], chosen[:, :], score[:, :], ALU.mult)
                elif i == 20:
                    ins = V.tensor_reduce(total[:, :], ties, AX_X, ALU.add)
                elif i == 21:
                    ins = V.tensor_scalar(total[:, :], total[:, :], 1e-20, None, ALU.add)
                elif i == 22:
                    ins = V.reciprocal(inv[:, :], total[:, :])
                elif i == 23:
                    ins = V.tensor_scalar(inv[:, :], inv[:, :], SCALE, None, ALU.mult)
                elif i == 24:
                    ins = tt(ties, ties, inv[:, :].rearrange("p (t a) -> p t a", a=1).to_broadcast([P, CT, E]), ALU.mult)
                elif i == 25:
                    ins = V.tensor_copy(mix[:, :, 0, :].bitcast(F32R), ties)
                elif i == 26:
                    ins = tt(mix[:, :, 1, :], ties, mix[:, :, 0, :], ALU.subtract)
                else:
                    return
                ins.then_inc(route_step, 1)

            def gated_product(c, p):
                dve.wait_ge(silu_done, SLOTS * c + p + 1)
                dve.wait_ge(up_done, SLOTS * c + p + 1)
                bank = mix_bank[1] if p == PAIRS else up_bank[p % 2]
                nc.vector.tensor_tensor(hid[:, p % 3, :], bank[:, :], hid[:, p % 3, :], ALU.mult).then_inc(gated, 1)

            def weighted_product(c, p):
                dve.wait_ge(gated, SLOTS * c + p + 1)
                dve.wait_ge(mix_done, PAIRS * c + p + 1)
                nc.vector.tensor_tensor(hid[:, p % 3, :], mix_bank[p % 2][:, :], hid[:, p % 3, :],
                                        ALU.mult).then_inc(weighted, 1)

            def update_x(c):
                dve.wait_ge(y_turned, c + 1)
                t = x_all[:, tiles(c), :].rearrange("p t d -> p (t d)")
                nc.vector.tensor_tensor(t, misc[:, :], t, ALU.add).then_inc(x_updated, 1)

            def slot(c, q, last):
                routing = not last and ROUTE_FROM <= q <= ROUTE_FROM + ROUTE_STEPS // 2
                if q < SLOTS or not last:
                    n, p = place(c, q)
                    gated_product(n, p)
                    if routing:
                        route(c + 1, 2 * (q - ROUTE_FROM))
                    if p < PAIRS:
                        weighted_product(n, p)
                    if routing:
                        route(c + 1, 2 * (q - ROUTE_FROM) + 1)
                if not last and q >= LEAD_F:
                    if q == 7:
                        ln_moments(c + 1)
                    if q == 8:
                        ln_apply(c + 1)
                    if q == 10:
                        xT_low(c + 1)
                if q == SLOTS + 4:
                    update_x(c)

            ln_moments(0)
            ln_apply(0)
            xT_low(0)
            for i in range(ROUTE_STEPS):
                route(0, i)
            run(dve, slot)

        @block.gpsimd
        def _(pool):
            def rstd_of(n):
                pool.wait_ge(ln_step, LN_STEPS * n + 2)
                nc.gpsimd.tensor_tensor(veps[:, :], moments[:, :, 1], w["eps"][:, 0:veps.shape[1]], ALU.add).then_inc(rstd_step, 1)
                pool.wait_ge(rstd_step, 2 * n + 1)
                if not (isinstance(n, int) and n == 0):
                    pool.wait_ge(ln_step, LN_STEPS * n)
                nc.gpsimd.tensor_tensor(rstd[:, :], veps[:, :], w["minus_half"][:, :], ALU.pow).then_inc(rstd_step, 1)

            def low(c, p):
                pool.wait_ge(hid_hi_done, SLOTS * c + p + 1)
                nc.gpsimd.tensor_tensor(hid_lo[:, p % 3, :], hid[:, p % 3, :],
                                        hid_hi[:, p % 3, :].bitcast(F32), ALU.subtract).then_inc(hid_lo_done, 1)

            def slot(c, q, last):
                if q < SLOTS or not last:
                    low(*place(c, q))
                if not last and q == 7:
                    rstd_of(c + 1)

            rstd_of(0)
            run(pool, slot)

        if out is not None:
            @block.sync
            def _(sp):
                with sp.Fori(0, NC) as c:
                    sp.wait_ge(x_updated, c + 1)
                    sp.dma_start(out[:, tiles(c), :], x_all[:, tiles(c), :]).then_inc(stored, 16)
                sp.wait_ge(stored, 16 * NC)


def attention(nc, w, x_all, psum):
    TB = SEQ // P
    NB = x_all.shape[1] // TB
    QUADS = H // 4
    STEPS = 2 * QUADS
    NPB = P + SEQ
    scores_late, scores_early = psum[0:2], psum[2]
    ring = psum[3:6]
    q_bank = v_bank = ring[0]
    k_bank = ring[1]
    turn_bank = (ring[2], ring[1], ring[2])
    o_bank, acc = psum[6], psum[7]
    with ExitStack() as ctx:
        def sb(name, shape, dt=F32):
            return ctx.enter_context(nc.sbuf_tensor("a_" + name, shape, dt))

        def sem(name):
            return ctx.enter_context(nc.semaphore("a_" + name))

        xn = sb("xn", [P, TB, D])
        stats, moments = sb("stats", [P, TB, 6]), sb("moments", [P, TB, 2])
        veps, rstd = sb("veps", [P, TB]), sb("rstd", [P, TB])
        hold = sb("hold", [P, 1])
        xT_hi = sb("xT_hi", [P, 2, SEQ], F32R)
        xT_lo = sb("xT_lo", [P, 2, SEQ], F32R)
        qT = sb("qT", [P, 2, 2, SEQ])
        kZ = sb("kZ", [P, 2, 2, 2, SEQ])
        v = sb("v", [P, 2, TB, 4 * HD])
        prob = sb("prob", [P, 2, 4 * NPB])
        probT = sb("probT", [P, 4 * NPB])
        oT = sb("oT", [P, 2, 2, SEQ])
        yT = sb("yT", [P, SEQ])
        top, bias = sb("top", [P, 2, 2, 2, 2]), sb("bias", [P, 2, 2, 2, 2])
        mass, inv = sb("mass", [P, 2, 2, 2, 2]), sb("inv", [P, 2, 2, 2, 2])

        zeroed = sem("zeroed")
        ln_step, rstd_step, xn_turned = sem("ln_step"), sem("rstd_step"), sem("xn_turned")
        xT_hi_done, xT_lo_done = sem("xT_hi_done"), sem("xT_lo_done")
        proj_done, q_read, k_read, v_read = sem("proj_done"), sem("q_read"), sem("k_read"), sem("v_read")
        scores_done, top_step, bias_done = sem("scores_done"), sem("top_step"), sem("bias_done")
        exp_done, inv_done, normed = sem("exp_done"), sem("inv_done"), sem("normed")
        prob_turned, probT_done = sem("prob_turned"), sem("probT_done")
        o_done, oT_done, out_done = sem("o_done"), sem("oT_done"), sem("out_done")
        yT_done, y_turned, x_updated = sem("yT_done"), sem("y_turned"), sem("x_updated")

        LN_STEPS = 3

        def at(c, k):
            return STEPS * c + k, 2 * c + k // QUADS

        def tiles(b):
            return slice(b * TB, (b + 1) * TB) if isinstance(b, int) else bass.ds(b * TB, TB)

        def run(engine, engine_slot):
            for k in range(LEAD_A):
                engine_slot(0, k, False)
            with engine.Fori(0, NB // 2 - 1) as c:
                for k in range(LEAD_A, STEPS + LEAD_A):
                    engine_slot(c, k, False)
            for k in range(LEAD_A, STEPS + LEAD_A):
                engine_slot(NB // 2 - 1, k, True)

        block = ctx.enter_context(nc.Block())

        @block.tensor
        def _(pe):
            def turn_xn(c, k):
                s, b = at(c, k)
                pe.wait_ge(ln_step, LN_STEPS * (b + 1) + 3)
                pe.wait_ge(v_read, s + 1)
                turn_xn_tiles()

            def turn_xn_tiles():
                for j in range(TB):
                    mm = nc.tensor.transpose(v_bank[:, j * P:(j + 1) * P], xn[:, j, :], w["ident"][:, :])
                mm.then_inc(xn_turned, 1)

            def project_qk(c, k, a, last):
                s, b = at(c, k)
                side, quad = k // QUADS % 2, k % QUADS
                xh, xl = xT_hi[:, side, :], xT_lo[:, side, :]
                if a == 0 and quad == 0:
                    pe.wait_ge(xT_lo_done, b + 1)
                if a == 0 and quad == 2 and k >= LEAD_A:
                    pe.wait_ge(x_updated, b)
                if a == 0 and quad == 3 and not (last and k == STEPS - 1):
                    pe.wait_ge(xT_lo_done, b + 2)
                if a == 0:
                    pe.wait_ge(v_read, s)
                elif not (isinstance(c, int) and c == 0 and k < 2):
                    pe.wait_ge(probT_done, 3 * s - 4)
                kind = ("pq", "pk")[a]
                for pair in range(2):
                    cols = slice((2 * quad + pair) * P, (2 * quad + pair + 1) * P)
                    o = (q_bank, k_bank)[a][:, pair * SEQ:(pair + 1) * SEQ]
                    hi, lo = w[kind + "_hi"][:, cols], w[kind + "_lo"][:, cols]
                    nc.tensor.matmul(o, hi, xh, start=True, stop=False)
                    nc.tensor.matmul(o, lo, xh, start=False, stop=False)
                    mm = nc.tensor.matmul(o, hi, xl, start=False, stop=True)
                mm.then_inc(proj_done, 1)

            def project_v(c, k):
                s, _ = at(c, k)
                side, quad = k // QUADS % 2, k % QUADS
                xh, xl = xT_hi[:, side, :], xT_lo[:, side, :]
                pe.wait_ge(q_read, s + 1)
                cols = slice(quad * 4 * HD, (quad + 1) * 4 * HD)
                hi, lo = w["pv_hi"][:, cols], w["pv_lo"][:, cols]
                for j in range(TB):
                    o = v_bank[:, j * SEQ:(j + 1) * SEQ]
                    t = slice(j * P, (j + 1) * P)
                    nc.tensor.matmul(o, xh[:, t], hi, start=True, stop=False)
                    nc.tensor.matmul(o, xh[:, t], lo, start=False, stop=False)
                    mm = nc.tensor.matmul(o, xl[:, t], hi, start=False, stop=True)
                mm.then_inc(proj_done, 1)

            def score_early(c, k):
                s, _ = at(c, k)
                i = k % 2
                pe.wait_ge(q_read, s + 1)
                pe.wait_ge(k_read, s + 1)
                pe.wait_ge(exp_done, 2 * s)
                for pair in range(2):
                    early = scores_early[:, pair * SEQ:(pair + 1) * SEQ]
                    nc.tensor.matmul(early, qT[:, i, pair, 0:P], kZ[:, i, pair, :, 0:P], start=True, stop=False)
                    mm = nc.tensor.matmul(early, w["ident_b"][:, :], w["mask"][:, :], start=False, stop=True)
                mm.then_inc(scores_done, 1)

            def score_late(c, k):
                i = k % 2
                for pair in range(2):
                    late = scores_late[pair]
                    nc.tensor.matmul(late[:, :], qT[:, i, pair, P:SEQ], kZ[:, i, pair, :, :], start=True, stop=False)
                    nc.tensor.matmul(late[:, :].rearrange("p (h n) -> p h n", h=2)[:, :, P:SEQ], w["ident_b"][:, :],
                                     w["mask"][:, :], start=False, stop=True).then_inc(scores_done, 1)

            def turn_prob(c, k, g, live):
                s, _ = at(c, k)
                pe.wait_ge(normed, 2 * s + (1 if g == 0 else 2))
                if g == 1 and live:
                    pe.wait_ge(k_read, s + 2)
                elif g == 2:
                    pe.wait_ge(probT_done, 3 * s + 1)
                elif not (isinstance(c, int) and c == 0 and k == 0):
                    pe.wait_ge(probT_done, 3 * s - g)
                bank = turn_bank[g]
                for j in range(4):
                    n = 4 * g + j
                    mm = nc.tensor.transpose(bank[:, j * P:(j + 1) * P], prob[:, k % 2, n * P:(n + 1) * P],
                                             w["ident"][:, :])
                mm.then_inc(prob_turned, 1)

            def weigh_values(c, k):
                s, _ = at(c, k)
                i = k % 2
                pe.wait_ge(v_read, s + 1)
                pe.wait_ge(oT_done, s)
                for pair in range(2):
                    pe.wait_ge(probT_done, 3 * s + 2 + pair)
                    for kb in range(2):
                        for h in range(2):
                            hh = 2 * pair + h
                            cols = slice(hh * NPB + kb * SEQ, hh * NPB + (SEQ if kb == 0 else NPB))
                            mm = nc.tensor.matmul(o_bank[h * HD:(h + 1) * HD, pair * SEQ + kb * P:(pair + 1) * SEQ],
                                                  v[:, i, kb, hh * HD:(hh + 1) * HD], probT[:, cols],
                                                  start=(kb == 0), stop=(kb == 1))
                mm.then_inc(o_done, 1)

            def output(c, k):
                s, b = at(c, k)
                quad = k % QUADS
                pe.wait_ge(oT_done, s + 1)
                if quad == 0:
                    pe.wait_ge(yT_done, b)
                for pair in range(2):
                    n = 2 * quad + pair
                    mm = nc.tensor.matmul(acc[:, 0:SEQ], w["po"][:, n * P:(n + 1) * P],
                                          oT[:, k % 2, pair, :], start=(n == 0), stop=(n == 2 * QUADS - 1))
                mm.then_inc(out_done, 1)

            def turn_y(c, k, live):
                s, b = at(c, k)
                pe.wait_ge(yT_done, b)
                if live:
                    pe.wait_ge(v_read, s + 1)
                for j in range(TB):
                    mm = nc.tensor.transpose(v_bank[:, j * P:(j + 1) * P], yT[:, j * P:(j + 1) * P],
                                             w["ident"][:, :])
                mm.then_inc(y_turned, 1)

            def slot(c, k, last):
                live = k < STEPS or not last
                soft = k >= 1 and (k - 1 < STEPS or not last)
                if live:
                    project_qk(c, k, 0, last)
                    project_qk(c, k, 1, last)
                if k >= 2 and (k - 2 < STEPS or not last):
                    output(c, k - 2)
                if live:
                    project_v(c, k)
                if soft:
                    turn_prob(c, k - 1, 0, live)
                if live:
                    score_early(c, k)
                if soft:
                    turn_prob(c, k - 1, 1, live)
                    turn_prob(c, k - 1, 2, live)
                if k % QUADS == 1 and k >= LEAD_A:
                    turn_y(c, k, live)
                if k % QUADS == 2 and not last:
                    turn_xn(c, k)
                if live:
                    score_late(c, k)
                if soft:
                    weigh_values(c, k - 1)

            pe.wait_ge(ln_step, LN_STEPS)
            turn_xn_tiles()
            run(pe, slot)

        @block.scalar
        def _(act):
            def xT_high(n, side):
                act.wait_ge(xn_turned, n + 1)
                nc.scalar.copy(xT_hi[:, side, :], v_bank[:, 0:SEQ]).then_inc(xT_hi_done, 1)

            def exps(c, k):
                s, _ = at(c, k)
                i = k % 2
                if not (isinstance(c, int) and c == 0 and k < 2):
                    act.wait_ge(prob_turned, 3 * s - 3)
                for pair in range(2):
                    act.wait_ge(bias_done, 2 * s + pair + 1)
                    early = scores_early[:, pair * SEQ:(pair + 1) * SEQ]
                    for h in range(2):
                        o = (2 * pair + h) * NPB
                        nc.scalar.activation(prob[:, i, o:o + P], early[:, h * P:(h + 1) * P], ACT.Exp,
                                             bias=bias[:, i, pair, 0, h:h + 1], scale=HD ** -0.5,
                                             accum_out=mass[:, i, pair, 0, h:h + 1])
                        e = nc.scalar.activation(prob[:, i, o + P:o + NPB],
                                                 scores_late[pair][:, h * SEQ:(h + 1) * SEQ], ACT.Exp,
                                                 bias=bias[:, i, pair, 1, h:h + 1], scale=HD ** -0.5,
                                                 accum_out=mass[:, i, pair, 1, h:h + 1])
                    e.then_inc(exp_done, 1)

            def copy_k(c, k):
                s, _ = at(c, k)
                if not (isinstance(c, int) and c == 0 and k < 2):
                    act.wait_ge(scores_done, 3 * s - 3)
                act.wait_ge(proj_done, 3 * s + 2)
                for h in range(2):
                    rows = slice(h * HD, (h + 1) * HD)
                    cp = nc.scalar.copy(kZ[rows, k % 2, :, h, :], k_bank[rows, :].rearrange("p (a n) -> p a n", a=2))
                cp.then_inc(k_read, 1)

            def copy_probT(c, k):
                s, _ = at(c, k)
                for g in range(3):
                    act.wait_ge(prob_turned, 3 * s + g + 1)
                    if g == 0:
                        act.wait_ge(o_done, s)
                    nc.scalar.copy(probT[:, g * 4 * P:(g + 1) * 4 * P],
                                   turn_bank[g][:, :]).then_inc(probT_done, 1)

            def copy_y(c, k):
                _, b = at(c, k)
                act.wait_ge(out_done, QUADS * b)
                nc.scalar.copy(yT[:, :], acc[:, 0:SEQ]).then_inc(yT_done, 1)

            def slot(c, k, last):
                soft = k >= 1 and (k - 1 < STEPS or not last)
                if soft:
                    exps(c, k - 1)
                if k < STEPS or not last:
                    copy_k(c, k)
                if k % QUADS == 1 and k >= LEAD_A:
                    copy_y(c, k)
                if soft:
                    copy_probT(c, k - 1)
                if k % QUADS == 2 and not last:
                    xT_high(at(c, k)[1] + 1, (k // QUADS + 1) % 2)

            xT_high(0, 0)
            run(act, slot)

        @block.vector
        def _(dve):
            def ln_moments(n):
                if not (isinstance(n, int) and n == 0):
                    dve.wait_ge(rstd_step, 2 * n)
                for j in range(TB):
                    i = nc.vector.bn_stats(stats[:, j, :], x_all[:, tiles(n), :][:, j, :])
                i.then_inc(ln_step, 1)
                dve.wait_ge(ln_step, LN_STEPS * n + 1)
                nc.vector.memset(hold[:, :], 0.0)
                for j in range(TB):
                    i = nc.vector.bn_aggr(moments[:, j, :], stats[:, j, :])
                i.then_inc(ln_step, 1)

            def ln_apply(n):
                dve.wait_ge(rstd_step, 2 * n + 2)
                dve.wait_ge(xn_turned, n)
                for j in range(TB):
                    i = nc.vector.tensor_scalar(xn[:, j, :], x_all[:, tiles(n), :][:, j, :], moments[:, j, 0:1],
                                                rstd[:, j:j + 1], ALU.subtract, ALU.mult)
                i.then_inc(ln_step, 1)

            def xT_low(n, side):
                dve.wait_ge(xT_hi_done, n + 1)
                nc.vector.tensor_tensor(xT_lo[:, side, :], v_bank[:, 0:SEQ], xT_hi[:, side, :].bitcast(F32),
                                        ALU.subtract).then_inc(xT_lo_done, 1)

            def copy_q(c, k):
                s, _ = at(c, k)
                if not (isinstance(c, int) and c == 0 and k < 2):
                    dve.wait_ge(scores_done, 3 * s - 3)
                dve.wait_ge(proj_done, 3 * s + 1)
                nc.vector.tensor_copy(qT[:, k % 2, :, :], q_bank[:, :].rearrange("p (a n) -> p a n", a=2))\
                    .then_inc(q_read, 1)

            def copy_v(c, k):
                s, _ = at(c, k)
                if not (isinstance(c, int) and c == 0 and k < 2):
                    dve.wait_ge(o_done, s - 1)
                dve.wait_ge(proj_done, 3 * s + 3)
                nc.vector.tensor_copy(v[:, k % 2, :, :], v_bank[:, :].rearrange("p (a n) -> p a n", a=TB))\
                    .then_inc(v_read, 1)

            def normalise(c, k, pair):
                s, _ = at(c, k)
                i = k % 2
                dve.wait_ge(exp_done, 2 * s + pair + 1)
                nc.vector.reciprocal(inv[:, i, pair, :, :], mass[:, i, pair, :, :]).then_inc(inv_done, 1)
                dve.wait_ge(inv_done, 2 * s + pair + 1)
                for h in range(2):
                    o = (2 * pair + h) * NPB
                    for late, (a, b) in enumerate(((o, o + P), (o + P, o + NPB))):
                        m = nc.vector.tensor_scalar(prob[:, i, a:b], prob[:, i, a:b],
                                                    inv[:, i, pair, late, h:h + 1], None, ALU.mult)
                m.then_inc(normed, 1)

            def copy_o(c, k):
                s, _ = at(c, k)
                if not (isinstance(c, int) and c == 0 and k < 2):
                    dve.wait_ge(out_done, s - 1)
                dve.wait_ge(o_done, s + 1)
                nc.vector.tensor_copy(oT[:, k % 2, :, :], o_bank[:, :].rearrange("p (a n) -> p a n", a=2))\
                    .then_inc(oT_done, 1)

            def maxima(c, k):
                s, _ = at(c, k)
                i = k % 2
                dve.wait_ge(scores_done, 3 * s + 1)
                early = scores_early[:, :].rearrange("p (a h n) -> p a h n", a=2, h=2)
                nc.vector.tensor_reduce(top[:, i, :, 0, :], early, AX_X, ALU.max)
                for pair in range(2):
                    dve.wait_ge(scores_done, 3 * s + pair + 2)
                    late = scores_late[pair][:, :].rearrange("p (h n) -> p h n", h=2)
                    nc.vector.tensor_reduce(top[:, i, pair, 1, :], late, AX_X, ALU.max).then_inc(top_step, 1)
                    dve.wait_ge(top_step, 2 * s + pair + 1)
                    nc.vector.tensor_scalar(bias[:, i, pair, :, :], top[:, i, pair, :, :], -HD ** -0.5, None,
                                            ALU.mult).then_inc(bias_done, 1)

            def update_x(c, k):
                _, b = at(c, k)
                dve.wait_ge(y_turned, b)
                t = x_all[:, tiles(b - 1), :].rearrange("p t d -> p (t d)")
                nc.vector.tensor_tensor(t, v_bank[:, 0:SEQ], t, ALU.add).then_inc(x_updated, 1)

            def slot(c, k, last):
                live = k < STEPS or not last
                soft = k >= 1 and (k - 1 < STEPS or not last)
                b = at(c, k)[1]
                if k >= 2 and (k - 2 < STEPS or not last):
                    copy_o(c, k - 2)
                if live:
                    copy_q(c, k)
                if soft:
                    normalise(c, k - 1, 0)
                    normalise(c, k - 1, 1)
                if k % QUADS == 1 and not last:
                    ln_moments(b + 1)
                if k % QUADS == 2 and not last:
                    ln_apply(b + 1)
                if live:
                    copy_v(c, k)
                if k % QUADS == 1 and k >= LEAD_A:
                    update_x(c, k)
                if k % QUADS == 2 and not last:
                    xT_low(b + 1, (k // QUADS + 1) % 2)
                if live:
                    maxima(c, k)

            for i in range(2):
                for h in range(2):
                    rows = slice((1 - h) * HD, (2 - h) * HD)
                    nc.vector.memset(kZ[rows, i, :, h, :], 0.0)
            ln_moments(0)
            ln_apply(0)
            xT_low(0, 0)
            run(dve, slot)

        @block.gpsimd
        def _(pool):
            def rstd_of(n):
                pool.wait_ge(ln_step, LN_STEPS * n + 2)
                nc.gpsimd.tensor_tensor(veps[:, :], moments[:, :, 1], w["eps"][:, 0:veps.shape[1]], ALU.add).then_inc(rstd_step, 1)
                pool.wait_ge(rstd_step, 2 * n + 1)
                nc.gpsimd.tensor_tensor(rstd[:, :], veps[:, :], w["minus_half"][:, 0:TB], ALU.pow)\
                    .then_inc(rstd_step, 1)

            rstd_of(0)
            with pool.Fori(1, NB) as n:
                rstd_of(n)


def macaron(nc, x, P_q, P_k, P_v, P_o, gate_w, gate_bias, We_gate, We_up, We_down, Ws_gate, Ws_up, Ws_down, out):
    B, M, _ = x.shape
    tiles = B * M // P
    dr = {"pq": P_q, "pk": P_k, "pv": P_v, "po": P_o, "gw": gate_w, "wg": We_gate, "wu": We_up, "wd": We_down,
          "sg": Ws_gate, "su": Ws_up, "sd": Ws_down,
          "gb": gate_bias.rearrange("(a e) -> a e", a=1).to_broadcast([P, E])}
    x_v = x.rearrange("b (t p) d -> p (b t) d", p=P)
    out_v = out.rearrange("b (t p) d -> p (b t) d", p=P)
    with ExitStack() as ctx:
        def sb(name, shape, dt=F32):
            return ctx.enter_context(nc.sbuf_tensor(name, shape, dt))

        x_all = sb("x_all", [P, tiles, D])
        w = {}
        for kind in ("wg", "wu", "wd"):
            for part in ("_hi", "_lo"):
                w[kind + part] = sb(kind + part, [P, SLOTS * P], F32R)
        for kind in ("pq", "pk", "pv"):
            for part in ("_hi", "_lo"):
                w[kind + part] = sb(kind + part, [P, H * HD], F32R)
        w["po"] = sb("po", [P, H * HD])
        w["gw_hi"], w["gw_lo"] = sb("gw_hi", [P, P], F32R), sb("gw_lo", [P, P], F32R)
        w["sel"] = sb("sel", [P, PAIRS * P], F32R)
        w["bias"] = sb("gate_bias", [P, E])
        w["ident"] = sb("ident", [P, P])
        w["ident_b"] = sb("ident_b", [P, P], BF16)
        w["mask"] = sb("mask", [P, 2 * P], BF16)
        w["earlier"] = sb("earlier", [P, E])
        w["minus_half"] = sb("minus_half", [P, CT])
        w["eps"] = sb("eps", [P, CT])
        psum = [ctx.enter_context(nc.psum_tensor(f"bank{i}", [P, 512], F32)) for i in range(8)]

        setup(nc, w, x_v, x_all, dr, psum)
        ffn(nc, "f1_", w, x_all, psum, None)
        attention(nc, w, x_all, psum)
        ffn(nc, "f2_", w, x_all, psum, out_v)


_INS = ["L0_attn_x", "L0_attn_P_q", "L0_attn_P_k", "L0_attn_P_v", "L0_attn_P_o", "L0_ffn_gate_w", "L0_ffn_gate_bias",
        "L0_ffn_We_gate", "L0_ffn_We_up", "L0_ffn_We_down", "L0_ffn_Ws_gate", "L0_ffn_Ws_up", "L0_ffn_Ws_down"]


def kernel(**inputs):
    import numpy as _np
    import concourse.bacc as _bacc
    from concourse import mybir as _mybir
    from concourse.bass_utils import run_bass_kernel_spmd as _run

    nc = _bacc.Bacc("TRN2", target_bir_lowering=False, num_devices=1)
    arrays, args = {}, []
    for name in _INS:
        a = _np.ascontiguousarray(inputs[name])
        arrays[f"in_{name}"] = a
        args.append(nc.dram_tensor(f"in_{name}", a.shape, _mybir.dt.from_np(a.dtype), kind="ExternalInput").ap())
    x = arrays["in_L0_attn_x"]
    out = nc.dram_tensor("out_0", x.shape, _mybir.dt.from_np(x.dtype), kind="ExternalOutput").ap()
    macaron(nc, *args, out)
    r = _run(nc, [arrays], core_ids=[0])
    return r.results[0]["out_0"]
```

```python
from contextlib import ExitStack

import concourse.bass as bass
from concourse import mybir

F32 = mybir.dt.float32
F32R = mybir.dt.float32r
BF16 = mybir.dt.bfloat16
ALU = mybir.AluOpType
ACT = mybir.ActivationFunctionType
AX_X = mybir.AxisListType.X

P = 128
D = 128
E = 64
F = 64
NG = 8
TOPK_GROUPS = 4
PAIRS = E // 2
SLOTS = PAIRS + 1
H = 16
HD = 64
SEQ = 256
CT = 4
CHUNK = CT * P
SCALE = 2.5
LN_EPS = 1e-5
OFF = -3.0e38
TAKEN = -3.3e38
MASKED = -1.0e30
LN_STEPS = 3
ROUTE_STEPS = 25
LEAD_F = 6
GROUP = 8
SPREAD = 4
PIECES_AFTER = {1: (6, 7, 8), 2: (9, 10, 11), 3: (12, 13, 14), 5: (15, 16, 17)}
LANDINGS = 6
SPLITS = {3: (3,), 4: (4,), 5: (5,), 8: (6,), 10: (7,), 11: (8,), 12: (9,), 13: (10,), 14: (11,),
          28: (12, 13, 14), 30: (15,), 31: (16,), 32: (17,)}
LEAD_A = 3


def weight_pieces(w, dr):
    pieces = []
    n = GROUP * P

    def add(hi, lo, src):
        rows, cols = hi.shape
        pieces.append((w["landing"][0:rows, len(pieces) % LANDINGS, 0:cols], hi, lo, src))

    for j in range(PAIRS // GROUP):
        c = slice(j * n, (j + 1) * n)
        experts = slice(2 * j * GROUP, 2 * (j + 1) * GROUP)
        for kind in ("wg", "wu"):
            add(w[kind + "_hi"][:, c], w[kind + "_lo"][:, c], dr[kind][experts].rearrange("e d f -> d e f"))
        add(w["wd_hi"][:, c], w["wd_lo"][:, c], dr["wd"][experts].rearrange("(n t) f h -> (t f) n h", t=2))
    c = slice(PAIRS * P, PAIRS * P + F)
    for i, (kind, src) in enumerate((("wg", "sg"), ("wu", "su"))):
        pieces.append((w["landing"][:, 0, i * F:(i + 1) * F], w[kind + "_hi"][:, c], w[kind + "_lo"][:, c], dr[src]))
    c = slice(PAIRS * P, PAIRS * P + D)
    pieces.append((w["landing"][0:F, 0, 2 * F:2 * F + D], w["wd_hi"][0:F, c], w["wd_lo"][0:F, c], dr["sd"]))
    for i, kind in enumerate(("pq", "pk", "pv")):
        pieces.append((w["landing"][:, 2 * i + 1, :], w[kind + "_hi"][:, :], w[kind + "_lo"][:, :],
                       dr[kind].rearrange("h d k -> d h k")))
    return pieces


class Parts:
    pass


def router_buffers(ctx, nc):
    def sb(name, shape, dt=F32):
        return ctx.enter_context(nc.sbuf_tensor("r_" + name, shape, dt))

    xn = sb("xn", [P, CT, D])
    stats = sb("stats", [P, CT, 6])
    moments = sb("moments", [P, CT, 2])
    veps = sb("veps", [P, CT])
    rstd = sb("rstd", [P, CT])
    hold = sb("hold", [P, 1])
    xT_hi = sb("xT_hi", [P, 2 * CHUNK], F32R)
    xT_lo = sb("xT_lo", [P, 2 * CHUNK], F32R)
    mixT = sb("mixT", [P, CHUNK // 2])
    yT = sb("yT", [P, CHUNK])
    score = sb("score", [P, CT * E])
    biased = sb("biased", [P, CT * E])
    kept = sb("kept", [P, CT * E])
    chosen = sb("chosen", [P, CT * E])
    mix = sb("mix", [P, CT * E])
    h4, l4 = sb("h4", [P, CT * NG, 4]), sb("l4", [P, CT * NG, 4])
    h2, m2, l2 = (sb(n, [P, CT * NG, 2]) for n in ("h2", "m2", "l2"))
    h1, m1, l1 = (sb(n, [P, CT * NG]) for n in ("h1", "m1", "l1"))
    gscore, rank, keep, drop = (sb(n, [P, CT * NG]) for n in ("gscore", "rank", "keep", "drop"))
    top8 = sb("top8", [P, CT, 8])
    total, inv = sb("total", [P, CT]), sb("inv", [P, CT])
    parts = Parts()
    parts.xn, parts.stats, parts.moments, parts.veps = xn, stats, moments, veps
    parts.rstd, parts.hold, parts.xT_hi, parts.xT_lo = rstd, hold, xT_hi, xT_lo
    parts.mixT, parts.yT, parts.score, parts.biased = mixT, yT, score, biased
    parts.kept, parts.chosen, parts.mix, parts.h4 = kept, chosen, mix, h4
    parts.l4, parts.h2, parts.m2, parts.l2 = l4, h2, m2, l2
    parts.h1, parts.m1, parts.l1, parts.gscore = h1, m1, l1, gscore
    parts.rank, parts.keep, parts.drop, parts.top8 = rank, keep, drop, top8
    parts.total, parts.inv = total, inv
    return parts


def router(ctx, nc, tag, w, x_all, mix_rows, b):
    def sem(name):
        return ctx.enter_context(nc.semaphore(tag + name))

    xn, xT_hi, xT_lo, mixT, yT, score, mix = b.xn, b.xT_hi, b.xT_lo, b.mixT, b.yT, b.score, b.mix
    ln_step, rstd_step, xn_turned = sem("ln_step"), sem("rstd_step"), sem("xn_turned")
    xT_hi_done, xT_lo_done = sem("xT_hi_done"), sem("xT_lo_done")
    logits_done, score_done, route_step = sem("logits_done"), sem("score_done"), sem("route_step")
    mix_turned, mixT_done, mix_stored = sem("mix_turned"), sem("mixT_done"), sem("mix_stored")

    def on_tensor(pe, misc):
        def turn_xn(n):
            pe.wait_ge(ln_step, LN_STEPS * n + 3)
            for j in range(CT):
                mm = nc.tensor.transpose(misc[:, j * P:(j + 1) * P], xn[:, j, :], w["ident"][:, :])
            mm.then_inc(xn_turned, 1)

        def logits(n):
            pe.wait_ge(xT_lo_done, n + 1)
            for a, (wk, xt) in enumerate((("gw_hi", xT_hi), ("gw_lo", xT_hi), ("gw_hi", xT_lo))):
                mm = nc.tensor.matmul(misc[:, :], w[wk][:, :], xt[:, half(n, CHUNK)],
                                      start=(a == 0), stop=(a == 2))
            mm.then_inc(logits_done, 1)

        def turn_logits(n):
            pe.wait_ge(score_done, 2 * n + 1)
            for j in range(CT):
                mm = nc.tensor.transpose(misc[:, j * P:(j + 1) * P], yT[:, j * P:(j + 1) * P], w["ident"][:, :])
            mm.then_inc(logits_done, 1)

        def turn_mix(n):
            pe.wait_ge(route_step, ROUTE_STEPS * (n + 1))
            pe.wait_ge(score_done, 2 * n + 2)
            for j in range(CT // 2):
                mm = nc.tensor.transpose(misc[:, j * P:(j + 1) * P], mix[:, j * P:(j + 1) * P],
                                         w["ident"][:, :])
            mm.then_inc(mix_turned, 1)

        return turn_xn, logits, turn_logits, turn_mix

    def on_scalar(act, misc):
        def xT_high(n):
            act.wait_ge(xn_turned, n + 1)
            nc.scalar.copy(xT_hi[:, half(n, CHUNK)], misc[:, :]).then_inc(xT_hi_done, 1)

        def sigmoid(n):
            act.wait_ge(logits_done, 2 * n + 1)
            nc.scalar.activation(yT[:, :], misc[:, :], ACT.Sigmoid).then_inc(score_done, 1)

        def copy_score(n):
            act.wait_ge(logits_done, 2 * n + 2)
            if not (isinstance(n, int) and n == 0):
                act.wait_ge(route_step, ROUTE_STEPS * n)
            nc.scalar.copy(score[:, :].rearrange("p (t e) -> p t e", e=E),
                           misc[:, :].rearrange("p (t n) -> p t n", n=P)[:, :, 0:E]).then_inc(score_done, 1)

        def copy_mixT(n):
            act.wait_ge(mix_turned, n + 1)
            if not (isinstance(n, int) and n == 0):
                act.wait_ge(mix_stored, 32 * n)
            nc.scalar.copy(mixT[:, :], misc[:, 0:CHUNK // 2]).then_inc(mixT_done, 1)

        return xT_high, sigmoid, copy_score, copy_mixT

    def on_vector(dve, misc):
        stats, moments, rstd, hold = b.stats, b.moments, b.rstd, b.hold
        biased, kept, chosen, top8, total, inv = b.biased, b.kept, b.chosen, b.top8, b.total, b.inv
        h4, l4, h2, m2, l2, h1, m1, l1 = b.h4, b.l4, b.h2, b.m2, b.l2, b.h1, b.m1, b.l1
        gscore, rank, keep, drop = b.gscore, b.rank, b.keep, b.drop

        def v8(t):
            return t[:, :].rearrange("p (g e) -> p g e", e=E // NG)

        def by_tile(t, n):
            return t[:, :].rearrange("p (t n) -> p t n", n=n)

        def by_group(t):
            return t[:, :].rearrange("p (g a) -> p g a", a=1).to_broadcast([P, CT * NG, E // NG])

        def ln_moments(n):
            if not (isinstance(n, int) and n == 0):
                dve.wait_ge(rstd_step, 2 * n)
            for j in range(CT):
                i = nc.vector.bn_stats(stats[:, j, :], x_all[:, tiles(n), :][:, j, :])
            i.then_inc(ln_step, 1)
            dve.wait_ge(ln_step, LN_STEPS * n + 1)
            nc.vector.memset(hold[:, :], 0.0)
            for j in range(CT):
                i = nc.vector.bn_aggr(moments[:, j, :], stats[:, j, :])
            i.then_inc(ln_step, 1)

        def ln_apply(n):
            dve.wait_ge(rstd_step, 2 * n + 2)
            dve.wait_ge(xn_turned, n)
            for j in range(CT):
                i = nc.vector.tensor_scalar(xn[:, j, :], x_all[:, tiles(n), :][:, j, :], moments[:, j, 0:1],
                                            rstd[:, j:j + 1], ALU.subtract, ALU.mult)
            i.then_inc(ln_step, 1)

        def xT_low(n):
            dve.wait_ge(xT_hi_done, n + 1)
            nc.vector.tensor_tensor(xT_lo[:, half(n, CHUNK)], misc[:, :],
                                    xT_hi[:, half(n, CHUNK)].bitcast(F32), ALU.subtract).then_inc(xT_lo_done, 1)

        def route(n, i):
            tt, V = nc.vector.tensor_tensor, nc.vector
            g8 = [P, CT, NG, NG]
            gs = by_tile(gscore, NG)
            best, ties = by_tile(kept, E), by_tile(chosen, E)
            if i == 0:
                dve.wait_ge(score_done, 2 * n + 2)
                dve.wait_ge(mix_turned, n)
            else:
                dve.wait_ge(route_step, ROUTE_STEPS * n + i)
            if i == 0:
                ins = tt(by_tile(biased, E), by_tile(score, E),
                         w["bias"][:, :].rearrange("p (a e) -> p a e", a=1).to_broadcast([P, CT, E]), ALU.add)
            elif i == 1:
                tt(h4[:, :, :], v8(biased)[:, :, 0:4], v8(biased)[:, :, 4:8], ALU.max)
                ins = tt(l4[:, :, :], v8(biased)[:, :, 0:4], v8(biased)[:, :, 4:8], ALU.min)
            elif i == 2:
                tt(h2[:, :, :], h4[:, :, 0:2], h4[:, :, 2:4], ALU.max)
                tt(m2[:, :, :], h4[:, :, 0:2], h4[:, :, 2:4], ALU.min)
                ins = tt(l2[:, :, :], l4[:, :, 0:2], l4[:, :, 2:4], ALU.max)
            elif i == 3:
                tt(h1[:, :], h2[:, :, 0], h2[:, :, 1], ALU.max)
                tt(m1[:, :], h2[:, :, 0], h2[:, :, 1], ALU.min)
                ins = tt(l2[:, :, :], l2[:, :, :], m2[:, :, :], ALU.max)
            elif i == 4:
                ins = tt(l1[:, :], l2[:, :, 0], l2[:, :, 1], ALU.max)
            elif i == 5:
                ins = tt(l1[:, :], l1[:, :], m1[:, :], ALU.max)
            elif i == 6:
                ins = tt(gscore[:, :], h1[:, :], l1[:, :], ALU.add)
            elif i == 7:
                ins = tt(best.rearrange("p t (g h) -> p t g h", g=NG),
                         gs.rearrange("p t (a g) -> p t a g", a=1).to_broadcast(g8),
                         gs.rearrange("p t (g a) -> p t g a", a=1).to_broadcast(g8), ALU.is_gt)
            elif i == 8:
                ins = tt(ties.rearrange("p t (g h) -> p t g h", g=NG),
                         gs.rearrange("p t (a g) -> p t a g", a=1).to_broadcast(g8),
                         gs.rearrange("p t (g a) -> p t g a", a=1).to_broadcast(g8), ALU.is_equal)
            elif i == 9:
                ins = tt(ties, ties, w["earlier"][:, :].rearrange("p (a e) -> p a e", a=1).to_broadcast([P, CT, E]),
                         ALU.mult)
            elif i == 10:
                ins = tt(kept[:, :], kept[:, :], chosen[:, :], ALU.add)
            elif i == 11:
                ins = V.tensor_reduce(rank[:, :], v8(kept), AX_X, ALU.add)
            elif i == 12:
                ins = V.tensor_scalar(keep[:, :], rank[:, :], float(TOPK_GROUPS), None, ALU.is_lt)
            elif i == 13:
                ins = V.tensor_scalar(drop[:, :], keep[:, :], -OFF, OFF, ALU.mult, ALU.add)
            elif i == 14:
                ins = tt(v8(kept), v8(biased), by_group(keep), ALU.mult)
            elif i == 15:
                ins = tt(v8(kept), v8(kept), by_group(drop), ALU.add)
            elif i == 16:
                V.memset(hold[:, :], 0.0)
                for j in range(CT):
                    ins = V.max(top8[:, j, :], kept[:, j * E:(j + 1) * E])
            elif i == 17:
                V.memset(hold[:, :], 0.0)
                for j in range(CT):
                    ins = V.match_replace(chosen[:, j * E:(j + 1) * E], top8[:, j, :],
                                          kept[:, j * E:(j + 1) * E], TAKEN)
            elif i == 18:
                ins = tt(chosen[:, :], chosen[:, :], kept[:, :], ALU.not_equal)
            elif i == 19:
                ins = tt(chosen[:, :], chosen[:, :], score[:, :], ALU.mult)
            elif i == 20:
                ins = V.tensor_reduce(total[:, :], ties, AX_X, ALU.add)
            elif i == 21:
                ins = V.tensor_scalar(total[:, :], total[:, :], 1e-20, None, ALU.add)
            elif i == 22:
                ins = V.reciprocal(inv[:, :], total[:, :])
            elif i == 23:
                ins = V.tensor_scalar(inv[:, :], inv[:, :], SCALE, None, ALU.mult)
            elif i == 24:
                ins = tt(by_tile(mix, E), ties,
                         inv[:, :].rearrange("p (t a) -> p t a", a=1).to_broadcast([P, CT, E]), ALU.mult)
            else:
                return
            ins.then_inc(route_step, 1)

        return ln_moments, ln_apply, xT_low, route

    def on_gpsimd(pool):
        veps, moments, rstd = b.veps, b.moments, b.rstd

        def rstd_of(n):
            pool.wait_ge(ln_step, LN_STEPS * n + 2)
            nc.gpsimd.tensor_tensor(veps[:, :], moments[:, :, 1], w["eps"][:, 0:veps.shape[1]], ALU.add)\
                .then_inc(rstd_step, 1)
            pool.wait_ge(rstd_step, 2 * n + 1)
            if not (isinstance(n, int) and n == 0):
                pool.wait_ge(ln_step, LN_STEPS * n)
            nc.gpsimd.tensor_tensor(rstd[:, :], veps[:, :], w["minus_half"][:, :], ALU.pow).then_inc(rstd_step, 1)

        return rstd_of

    def on_sync(sp):
        def store_mix(n):
            sp.wait_ge(mixT_done, n + 1)
            row = mix_rows[n] if isinstance(n, int) else mix_rows[bass.ds(n, 1)].rearrange("a e t -> (a e) t")
            row = row.rearrange("e (j h t) -> e h j t", h=2, t=P)
            for h in range(2):
                sp.dma_start(row[:, h, :, :], mixT[h * E:(h + 1) * E, :].rearrange("e (j t) -> e j t", t=P))\
                    .then_inc(mix_stored, 16)

        return store_mix

    parts = Parts()
    parts.ln_step, parts.rstd_step, parts.xn_turned, parts.xT_hi_done = ln_step, rstd_step, xn_turned, xT_hi_done
    parts.xT_lo_done, parts.logits_done, parts.score_done = xT_lo_done, logits_done, score_done
    parts.route_step = route_step
    parts.mix_turned, parts.mixT_done, parts.mix_stored, parts.on_tensor = mix_turned, mixT_done, mix_stored, on_tensor
    parts.on_scalar, parts.on_vector, parts.on_gpsimd, parts.on_sync = on_scalar, on_vector, on_gpsimd, on_sync
    return parts


def tiles(c):
    return slice(c * CT, (c + 1) * CT) if isinstance(c, int) else bass.ds(c * CT, CT)


def half(c, width):
    o = (c % 2) * width
    return slice(o, o + width) if isinstance(c, int) else bass.ds(o, width)


def ffn(nc, tag, w, x_all, psum, mix_rows, b, route_by, rows=None, load=None, out=None):
    NC = x_all.shape[1] // CT
    gate_bank, up_bank = psum[0:3], psum[3:6]
    acc, misc = psum[6], psum[7]
    with ExitStack() as ctx:
        def sb(name, shape, dt=F32):
            return ctx.enter_context(nc.sbuf_tensor(tag + name, shape, dt))

        def sem(name):
            return ctx.enter_context(nc.semaphore(tag + name))

        mix_wide = sb("mix_wide", [P, 2, SPREAD, CHUNK])
        hid = sb("hid", [P, 3, CHUNK])
        hid_hi = sb("hid_hi", [P, 3, CHUNK], F32R)
        hid_lo = sb("hid_lo", [P, 3, CHUNK], F32R)
        gate_done, up_done, down_done = sem("gate_done"), sem("up_done"), sem("down_done")
        silu_done, gated, weighted = sem("silu_done"), sem("gated"), sem("weighted")
        hid_hi_done, hid_lo_done = sem("hid_hi_done"), sem("hid_lo_done")
        yT_done, y_turned, x_updated = sem("yT_done"), sem("y_turned"), sem("x_updated")
        mix_spread = [sem("mix_spread0"), sem("mix_spread1")]
        first_spread = sem("first_spread")
        stored = sem("stored")

        if load:
            x, dr = load
            pieces = weight_pieces(w, dr)
            gw_raw = sb("gw_raw", [E, D])
            attn_piece, shared_piece = len(pieces) - 3, len(pieces) - 6
            landed = [sem(f"landed{n}") for n in range(len(pieces))]
            x_first, x_rest, gw_landed, bias_landed, po_landed = (
                sem(n) for n in ("x_first", "x_rest", "gw_landed", "bias_landed", "po_landed"))
            hi_split, lo_split, gw_turned, gw_split = sem("hi_split"), sem("lo_split"), sem("gw_turned"), sem("gw_split")
            po_turned, po_copied = sem("po_turned"), sem("po_copied")
            const_step, ident_ready, earlier_ready, padded, wd_padded = (
                sem(n) for n in ("const_step", "ident_ready", "earlier_ready", "padded", "wd_padded"))

        GROUPS = PAIRS // SPREAD
        xT_hi, xT_lo, yT = b.xT_hi, b.xT_lo, b.yT
        xT_lo_done, score_done, mixT_done, mix_stored = (
            route_by.xT_lo_done, route_by.score_done, route_by.mixT_done, route_by.mix_stored)
        MOMENTS, APPLY, TURN_XN, LOGITS, TURN_LOGITS, ROUTE_FROM, TURN_MIX = 6, 7, 9, 11, 13, 14, 27
        TURN_PO = (20, 22)

        def place(c, q):
            return (c, q) if q < SLOTS else (c + 1, q - SLOTS)

        def splits(c, q):
            return SPLITS.get(q, ()) if load and isinstance(c, int) and c == 0 else ()

        def body(engine_slot, c, last):
            for q in range(LEAD_F, SLOTS + LEAD_F):
                if not last or q < SLOTS + 5:
                    engine_slot(c, q, last)

        def run(engine, engine_slot):
            for q in range(3, LEAD_F):
                engine_slot(0, q, False)
            if load:
                body(engine_slot, 0, False)
            with engine.Fori(1 if load else 0, NC - 1) as c:
                body(engine_slot, c, False)
            body(engine_slot, NC - 1, True)

        block = ctx.enter_context(nc.Block())

        @block.tensor
        def _(pe):
            turn_xn, logits, turn_logits, turn_mix = route_by.on_tensor(pe, misc)

            turn_row = rows.on_tensor(pe, misc) if rows else None

            def turn_gw():
                pe.wait_ge(ident_ready, 1)
                pe.wait_ge(gw_landed, 16)
                nc.tensor.transpose(acc[:, 0:E], gw_raw[:, :], w["ident"][0:E, 0:E]).then_inc(gw_turned, 1)

            def turn_po(i):
                if i == 0:
                    pe.wait_ge(po_landed, 16)
                    pe.wait_ge(score_done, 4)
                else:
                    pe.wait_ge(po_copied, i)
                for j in range(4):
                    mm = nc.tensor.transpose(misc[:, j * P:(j + 1) * P], w["po"][:, (4 * i + j) * P:(4 * i + j + 1) * P],
                                             w["ident"][:, :])
                mm.then_inc(po_turned, 1)

            def three(bank, kind, p, rhs_hi, rhs_lo, start=True, stop=True):
                hi, lo = w[kind + "_hi"][:, p * P:(p + 1) * P], w[kind + "_lo"][:, p * P:(p + 1) * P]
                nc.tensor.matmul(bank[:, :], hi, rhs_hi, start=start, stop=False)
                nc.tensor.matmul(bank[:, :], lo, rhs_hi, start=False, stop=False)
                return nc.tensor.matmul(bank[:, :], hi, rhs_lo, start=False, stop=stop)

            def up(c, p):
                first = isinstance(c, int) and c == 0
                xh, xl = xT_hi[:, half(c, CHUNK)], xT_lo[:, half(c, CHUNK)]
                if p == 0:
                    pe.wait_ge(xT_lo_done, c + 1)
                g, u = gate_bank[p % 3], up_bank[p % 3]
                if p >= 3 or not first:
                    pe.wait_ge(silu_done, SLOTS * c + p - 2)
                if load and first and p % GROUP == 0:
                    pe.wait_ge(lo_split, 3 * (p // GROUP) + 1)
                    if p == PAIRS:
                        pe.wait_ge(padded, 2)
                three(g, "wg", p, xh, xl).then_inc(gate_done, 1)
                if p >= 3 or not first:
                    pe.wait_ge(gated, SLOTS * c + p - 2)
                if load and first and p % GROUP == 0:
                    pe.wait_ge(lo_split, 3 * (p // GROUP) + 2)
                three(u, "wu", p, xh, xl).then_inc(up_done, 1)

            def down(c, p):
                pe.wait_ge(hid_lo_done, SLOTS * c + p + 1)
                if p == 0 and not (isinstance(c, int) and c == 0):
                    pe.wait_ge(yT_done, c)
                if load and isinstance(c, int) and c == 0 and p % GROUP == 0:
                    pe.wait_ge(lo_split, 3 * (p // GROUP) + 3)
                    if p == PAIRS:
                        pe.wait_ge(wd_padded, 2)
                three(acc, "wd", p, hid_hi[:, p % 3, :], hid_lo[:, p % 3, :],
                      start=(p == 0), stop=(p == PAIRS)).then_inc(down_done, 1)

            def turn_y(c, last):
                pe.wait_ge(yT_done, c + 1)
                pe.wait_ge(mixT_done, c + 1 if last else c + 2)
                for j in range(CT):
                    mm = nc.tensor.transpose(misc[:, j * P:(j + 1) * P], yT[:, j * P:(j + 1) * P], w["ident"][:, :])
                mm.then_inc(y_turned, 1)

            def slot(c, q, last):
                if q < SLOTS or not last:
                    up(*place(c, q))
                if 3 <= q < SLOTS + 3 or (q >= SLOTS + 3 and not last):
                    down(*place(c, q - 3))
                if not last and q >= LEAD_F:
                    if q == TURN_XN:
                        turn_xn(c + 1)
                    if q == LOGITS:
                        logits(c + 1)
                    if q == TURN_LOGITS:
                        turn_logits(c + 1)
                    if load and isinstance(c, int) and c == 0 and q in TURN_PO:
                        turn_po(TURN_PO.index(q))
                    if q == TURN_MIX:
                        if load and isinstance(c, int) and c == 0:
                            pe.wait_ge(po_copied, 2)
                        turn_mix(c + 1)
                if rows and last and q == TURN_XN:
                    pe.wait_ge(rows.ln_step, LN_STEPS)
                    turn_row()
                if q == SLOTS + 4:
                    if rows and last:
                        pe.wait_ge(rows.xT_lo_done, 1)
                    turn_y(c, last)

            if load:
                turn_gw()
                turn_xn(0)
                pe.wait_ge(gw_split, 2)
                pe.wait_ge(padded, 1)
                logits(0)
                turn_logits(0)
            for p in range(3):
                up(0, p)
            if load:
                turn_mix(0)
            run(pe, slot)

        @block.scalar
        def _(act):
            xT_high, sigmoid, copy_score, copy_mixT = route_by.on_scalar(act, misc)

            row_high = rows.on_scalar(act, misc) if rows else None

            def weight_high(n):
                act.wait_ge(landed[n], 16)
                raw, hi, _, _ = pieces[n]
                nc.scalar.copy(hi, raw).then_inc(hi_split, 1)

            def copy_po(i):
                act.wait_ge(po_turned, i + 1)
                nc.scalar.copy(w["po"][:, 4 * i * P:4 * (i + 1) * P], misc[:, :]).then_inc(po_copied, 1)

            def silu(c, p):
                act.wait_ge(gate_done, SLOTS * c + p + 1)
                if p >= 3 or not (isinstance(c, int) and c == 0):
                    act.wait_ge(hid_lo_done, SLOTS * c + p - 2)
                nc.scalar.activation(hid[:, p % 3, :], gate_bank[p % 3][:, :], ACT.Silu).then_inc(silu_done, 1)

            def high(c, p):
                if p == PAIRS:
                    act.wait_ge(gated, SLOTS * (c + 1))
                else:
                    act.wait_ge(weighted, PAIRS * c + p + 1)
                if p >= 3 or not (isinstance(c, int) and c == 0):
                    act.wait_ge(down_done, SLOTS * c + p - 2)
                nc.scalar.copy(hid_hi[:, p % 3, :], hid[:, p % 3, :]).then_inc(hid_hi_done, 1)

            def copy_y(c):
                act.wait_ge(down_done, SLOTS * (c + 1))
                nc.scalar.mul(yT[:, :], acc[:, :], 0.5).then_inc(yT_done, 1)

            def slot(c, q, last):
                if q == SLOTS + 3:
                    copy_y(c)
                if q < SLOTS or not last:
                    silu(*place(c, q))
                if 1 <= q < SLOTS + 1 or (q >= SLOTS + 1 and not last):
                    high(*place(c, q - 1))
                if not last and q >= LEAD_F:
                    if q == TURN_XN:
                        xT_high(c + 1)
                    if q == LOGITS:
                        sigmoid(c + 1)
                    if q == TURN_LOGITS:
                        copy_score(c + 1)
                    if load and isinstance(c, int) and c == 0 and q in TURN_PO:
                        copy_po(TURN_PO.index(q))
                    if q == TURN_MIX:
                        copy_mixT(c + 1)
                if rows and last and q == TURN_XN:
                    row_high(0, 0)
                for n in splits(c, q):
                    weight_high(n)

            if load:
                act.wait_ge(gw_turned, 1)
                nc.scalar.copy(w["gw_hi"][:, 0:E], acc[:, 0:E]).then_inc(gw_split, 1)
                xT_high(0)
                weight_high(0)
                weight_high(1)
                sigmoid(0)
                copy_score(0)
                weight_high(2)
            for p in range(3):
                silu(0, p)
            if load:
                copy_mixT(0)
            high(0, 0)
            high(0, 1)
            run(act, slot)

        @block.vector
        def _(dve):
            ln_moments, ln_apply, xT_low, route = route_by.on_vector(dve, misc)

            row_moments, row_apply, row_low = rows.on_vector(dve, misc) if rows else (None, None, None)

            def weight_low(n):
                dve.wait_ge(hi_split, n + 1)
                raw, hi, lo, _ = pieces[n]
                nc.vector.tensor_tensor(lo, raw, hi.bitcast(F32), ALU.subtract).then_inc(lo_split, 1)

            def gated_product(c, p):
                dve.wait_ge(silu_done, SLOTS * c + p + 1)
                dve.wait_ge(up_done, SLOTS * c + p + 1)
                nc.vector.tensor_tensor(hid[:, p % 3, :], up_bank[p % 3][:, :], hid[:, p % 3, :], ALU.mult)\
                    .then_inc(gated, 1)

            def weighted_product(c, p):
                dve.wait_ge(gated, SLOTS * c + p + 1)
                g = p // SPREAD
                first = isinstance(c, int) and c == 0
                if first and p == 0:
                    dve.wait_ge(first_spread, 32)
                elif p % SPREAD == 0 or (first and p == 1):
                    dve.wait_ge(mix_spread[g % 2], 32 * (c * (GROUPS // 2) + g // 2 + 1))
                nc.vector.tensor_tensor(hid[:, p % 3, :], mix_wide[:, g % 2, p % SPREAD, :], hid[:, p % 3, :],
                                        ALU.mult).then_inc(weighted, 1)

            def update_x(c):
                dve.wait_ge(y_turned, c + 1)
                t = x_all[:, tiles(c), :].rearrange("p t d -> p (t d)")
                nc.vector.tensor_tensor(t, misc[:, :], t, ALU.add).then_inc(x_updated, 1)

            def slot(c, q, last):
                routing = not last and ROUTE_FROM <= q <= ROUTE_FROM + ROUTE_STEPS // 2
                if q < SLOTS or not last:
                    n, p = place(c, q)
                    gated_product(n, p)
                    if routing:
                        route(c + 1, 2 * (q - ROUTE_FROM))
                    if p < PAIRS:
                        weighted_product(n, p)
                    if routing:
                        route(c + 1, 2 * (q - ROUTE_FROM) + 1)
                if not last and q >= LEAD_F:
                    if q == MOMENTS:
                        if load and isinstance(c, int) and c == 0:
                            dve.wait_ge(x_rest, 16)
                        ln_moments(c + 1)
                    if q == APPLY:
                        ln_apply(c + 1)
                    if q == TURN_XN:
                        xT_low(c + 1)
                if q == SLOTS + 4:
                    update_x(c)
                if rows and last:
                    if q == MOMENTS:
                        row_moments(0)
                    if q == APPLY:
                        row_apply(0)
                    if q == TURN_XN:
                        row_low(0, 0)
                for n in splits(c, q):
                    weight_low(n)

            if load:
                for kind in ("wd_hi", "wd_lo"):
                    nc.vector.memset(w[kind][F:P, PAIRS * P:SLOTS * P].bitcast(F32), 0.0).then_inc(wd_padded, 1)
                dve.wait_ge(x_first, 16)
                ln_moments(0)
                ln_apply(0)
                dve.wait_ge(gw_split, 1)
                nc.vector.tensor_tensor(w["gw_lo"][:, 0:E], acc[:, 0:E], w["gw_hi"][:, 0:E].bitcast(F32),
                                        ALU.subtract).then_inc(gw_split, 1)
                xT_low(0)
                weight_low(0)
                weight_low(1)
                dve.wait_ge(bias_landed, 16)
                for i in range(ROUTE_STEPS):
                    if i == 9:
                        dve.wait_ge(earlier_ready, 1)
                    route(0, i)
                weight_low(2)
            for p in range(3):
                gated_product(0, p)
            for p in range(3):
                weighted_product(0, p)
            run(dve, slot)

        @block.gpsimd
        def _(pool):
            rstd_of = route_by.on_gpsimd(pool)

            def first_constants():
                nc.gpsimd.memset(w["ident"][:, :], 0.0).then_inc(const_step, 1)
                pool.wait_ge(const_step, 1)
                nc.gpsimd.affine_select(out=w["ident"][:, :], in_=w["ident"][:, :], compare_op=ALU.not_equal,
                                        fill=1.0, base=0, pattern=[[-1, P]], channel_multiplier=1)\
                    .then_inc(ident_ready, 1)
                nc.gpsimd.memset(w["minus_half"][:, :], -0.5).then_inc(const_step, 1)
                nc.gpsimd.memset(w["eps"][:, :], LN_EPS).then_inc(const_step, 1)
                nc.gpsimd.memset(w["gw_hi"][:, E:P].bitcast(F32), 0.0).then_inc(const_step, 1)
                nc.gpsimd.memset(w["gw_lo"][:, E:P].bitcast(F32), 0.0).then_inc(padded, 1)
                pool.wait_ge(const_step, 3)

            def other_constants():
                earlier = w["earlier"][:, :].rearrange("p (g h) -> p g h", g=NG)
                nc.gpsimd.memset(w["earlier"][:, :], 1.0).then_inc(const_step, 1)
                pool.wait_ge(const_step, 5)
                nc.gpsimd.affine_select(out=earlier, in_=earlier, compare_op=ALU.is_gt, fill=0.0, base=0,
                                        pattern=[[1, NG], [-1, NG]], channel_multiplier=0).then_inc(earlier_ready, 1)
                for kind in ("wg_hi", "wg_lo", "wu_hi", "wu_lo"):
                    m = nc.gpsimd.memset(w[kind][:, PAIRS * P + F:SLOTS * P].bitcast(F32), 0.0)
                m.then_inc(padded, 1)
                nc.gpsimd.memset(w["mask"][:, :], 0.0).then_inc(const_step, 1)
                nc.gpsimd.memset(w["ident_b"][:, :], 0.0).then_inc(const_step, 1)
                pool.wait_ge(const_step, 7)
                mask = w["mask"][:, :].rearrange("p (a b) -> p a b", a=2)
                nc.gpsimd.affine_select(out=mask, in_=mask, compare_op=ALU.is_ge, fill=MASKED, base=0,
                                        pattern=[[0, 2], [-1, P]], channel_multiplier=1)
                nc.gpsimd.affine_select(out=w["ident_b"][:, :], in_=w["ident_b"][:, :], compare_op=ALU.not_equal,
                                        fill=1.0, base=0, pattern=[[-1, P]], channel_multiplier=1)

            def low(c, p):
                pool.wait_ge(hid_hi_done, SLOTS * c + p + 1)
                nc.gpsimd.tensor_tensor(hid_lo[:, p % 3, :], hid[:, p % 3, :],
                                        hid_hi[:, p % 3, :].bitcast(F32), ALU.subtract).then_inc(hid_lo_done, 1)

            def slot(c, q, last):
                if q < SLOTS or not last:
                    low(*place(c, q))
                if not last and q == MOMENTS:
                    rstd_of(c + 1)
                if rows and last and q == MOMENTS:
                    rows.on_gpsimd(pool)(0)

            if load:
                first_constants()
                rstd_of(0)
                other_constants()
            for p in range(3):
                low(0, p)
            run(pool, slot)

        @block.sync
        def _(sp):
            store_mix = route_by.on_sync(sp)

            def spread(n, g):
                if g == 0:
                    sp.wait_ge(mix_stored, 32 * (n + 1))
                if g >= 2 or not (isinstance(n, int) and n == 0):
                    sp.wait_ge(weighted, PAIRS * n + SPREAD * (g - 1))
                rows = mix_rows[n] if isinstance(n, int) else mix_rows[bass.ds(n, 1)].rearrange("a e t -> (a e) t")
                group = rows[2 * SPREAD * g:2 * SPREAD * (g + 1), :].rearrange("(a p h) t -> a h p t", a=1, h=2)
                at = 0
                if isinstance(n, int) and n == 0 and g == 0:
                    at = 1
                    for h in range(2):
                        sp.dma_start(mix_wide[h * F:(h + 1) * F, 0, 0:1, :],
                                     group[:, h, 0:1, :].to_broadcast([F, 1, CHUNK])).then_inc(first_spread, 16)
                for h in range(2):
                    sp.dma_start(mix_wide[h * F:(h + 1) * F, g % 2, at:SPREAD, :],
                                 group[:, h, at:SPREAD, :].to_broadcast([F, SPREAD - at, CHUNK]))\
                        .then_inc(mix_spread[g % 2], 16)

            def store_x(c):
                sp.wait_ge(x_updated, c + 1)
                sp.dma_start(out[:, tiles(c), :], x_all[:, tiles(c), :]).then_inc(stored, 16)

            def piece(n):
                raw, _, _, src = pieces[n]
                if n >= attn_piece:
                    sp.wait_ge(lo_split, shared_piece)
                elif n >= shared_piece:
                    sp.wait_ge(lo_split, LANDINGS + 1)
                elif n >= LANDINGS:
                    sp.wait_ge(lo_split, n - LANDINGS + 1)
                if len(src.shape) == 3:
                    raw = raw.rearrange("p (a b) -> p a b", b=src.shape[2])
                sp.dma_start(raw, src).then_inc(landed[n], 16)

            def chunk(n):
                if load or not (isinstance(n, int) and n == 0):
                    store_mix(n)
                for g in range(GROUPS):
                    spread(n, g)
                    if g == 3 and out is not None and not (isinstance(n, int) and n == 0):
                        store_x(n - 1)
                    if load and isinstance(n, int) and n == 0:
                        if g == 1:
                            sp.dma_start(x_all[:, CT:, :], x[:, CT:, :]).then_inc(x_rest, 16)
                        for m in PIECES_AFTER.get(g, ()):
                            piece(m)
                        if g == 4:
                            sp.dma_start(w["po"][:, :].rearrange("d (h v) -> d h v", v=HD),
                                         dr["po"].rearrange("h d v -> d h v")).then_inc(po_landed, 16)

            if load:
                sp.dma_start(x_all[:, 0:CT, :], x[:, 0:CT, :]).then_inc(x_first, 16)
                sp.dma_start(gw_raw[:, :], dr["gw"]).then_inc(gw_landed, 16)
                sp.dma_start(w["bias"][:, :], dr["gb"]).then_inc(bias_landed, 16)
                for n in range(LANDINGS):
                    piece(n)
            chunk(0)
            with sp.Fori(1, NC) as n:
                chunk(n)
            if out is not None:
                store_x(NC - 1)
                sp.wait_ge(stored, 16 * NC)
            sp.wait_ge(mix_stored, 32 * NC)


def row_norm(ctx, nc, w, x_all):
    TB = SEQ // P

    def sb(name, shape, dt=F32):
        return ctx.enter_context(nc.sbuf_tensor("n_" + name, shape, dt))

    def sem(name):
        return ctx.enter_context(nc.semaphore("n_" + name))

    xn = sb("xn", [P, TB, D])
    stats, moments = sb("stats", [P, TB, 6]), sb("moments", [P, TB, 2])
    veps, rstd = sb("veps", [P, TB]), sb("rstd", [P, TB])
    hold = sb("hold", [P, 1])
    xT_hi = sb("xT_hi", [P, 2, SEQ], F32R)
    xT_lo = sb("xT_lo", [P, 2, SEQ], F32R)
    ln_step, rstd_step, xn_turned = sem("ln_step"), sem("rstd_step"), sem("xn_turned")
    xT_hi_done, xT_lo_done = sem("xT_hi_done"), sem("xT_lo_done")

    def row_tiles(b):
        return slice(b * TB, (b + 1) * TB) if isinstance(b, int) else bass.ds(b * TB, TB)

    def on_tensor(pe, bank):
        def turn_row():
            for j in range(TB):
                mm = nc.tensor.transpose(bank[:, j * P:(j + 1) * P], xn[:, j, :], w["ident"][:, :])
            mm.then_inc(xn_turned, 1)

        return turn_row

    def on_scalar(act, bank):
        def xT_high(n, side):
            act.wait_ge(xn_turned, n + 1)
            nc.scalar.copy(xT_hi[:, side, :], bank[:, 0:SEQ]).then_inc(xT_hi_done, 1)

        return xT_high

    def on_vector(dve, bank):
        def ln_moments(n):
            if not (isinstance(n, int) and n == 0):
                dve.wait_ge(rstd_step, 2 * n)
            for j in range(TB):
                i = nc.vector.bn_stats(stats[:, j, :], x_all[:, row_tiles(n), :][:, j, :])
            i.then_inc(ln_step, 1)
            dve.wait_ge(ln_step, LN_STEPS * n + 1)
            nc.vector.memset(hold[:, :], 0.0)
            for j in range(TB):
                i = nc.vector.bn_aggr(moments[:, j, :], stats[:, j, :])
            i.then_inc(ln_step, 1)

        def ln_apply(n):
            dve.wait_ge(rstd_step, 2 * n + 2)
            dve.wait_ge(xn_turned, n)
            for j in range(TB):
                i = nc.vector.tensor_scalar(xn[:, j, :], x_all[:, row_tiles(n), :][:, j, :], moments[:, j, 0:1],
                                            rstd[:, j:j + 1], ALU.subtract, ALU.mult)
            i.then_inc(ln_step, 1)

        def xT_low(n, side):
            dve.wait_ge(xT_hi_done, n + 1)
            nc.vector.tensor_tensor(xT_lo[:, side, :], bank[:, 0:SEQ], xT_hi[:, side, :].bitcast(F32),
                                    ALU.subtract).then_inc(xT_lo_done, 1)

        return ln_moments, ln_apply, xT_low

    def on_gpsimd(pool):
        def rstd_of(n):
            pool.wait_ge(ln_step, LN_STEPS * n + 2)
            nc.gpsimd.tensor_tensor(veps[:, :], moments[:, :, 1], w["eps"][:, 0:veps.shape[1]], ALU.add)\
                .then_inc(rstd_step, 1)
            pool.wait_ge(rstd_step, 2 * n + 1)
            nc.gpsimd.tensor_tensor(rstd[:, :], veps[:, :], w["minus_half"][:, 0:TB], ALU.pow)\
                .then_inc(rstd_step, 1)

        return rstd_of

    parts = Parts()
    parts.xT_hi, parts.xT_lo = xT_hi, xT_lo
    parts.ln_step, parts.xn_turned, parts.xT_lo_done = ln_step, xn_turned, xT_lo_done
    parts.on_tensor, parts.on_scalar, parts.on_vector, parts.on_gpsimd = on_tensor, on_scalar, on_vector, on_gpsimd
    return parts


def attention(nc, w, x_all, psum, rows, ahead):
    TB = SEQ // P
    NB = x_all.shape[1] // TB
    QUADS = H // 4
    STEPS = 2 * QUADS
    NPB = P + SEQ
    scores_late, scores_early = psum[0:2], psum[2]
    ring = psum[3:6]
    q_bank = v_bank = ring[0]
    k_bank = ring[1]
    turn_bank = (ring[2], ring[1], ring[2])
    o_bank, acc = psum[6], psum[7]
    with ExitStack() as ctx:
        def sb(name, shape, dt=F32):
            return ctx.enter_context(nc.sbuf_tensor("a_" + name, shape, dt))

        def sem(name):
            return ctx.enter_context(nc.semaphore("a_" + name))

        qT = sb("qT", [P, 2, 2, SEQ])
        kZ = sb("kZ", [P, 2, 2, 2, SEQ])
        v = sb("v", [P, 2, TB, 4 * HD])
        prob = sb("prob", [P, 4 * NPB])
        probT = sb("probT", [P, 4 * NPB])
        oT = sb("oT", [P, 2, 2, SEQ])
        yT = sb("yT", [P, SEQ])
        top, bias = sb("top", [P, 2, 2, 2, 2]), sb("bias", [P, 2, 2, 2, 2])
        mass, inv = sb("mass", [P, 2, 2, 2, 2]), sb("inv", [P, 2, 2, 2, 2])

        xT_hi, xT_lo, ln_step, xT_lo_done = rows.xT_hi, rows.xT_lo, rows.ln_step, rows.xT_lo_done
        proj_done, q_read, k_read, v_read = sem("proj_done"), sem("q_read"), sem("k_read"), sem("v_read")
        scores_done, top_step, bias_done = sem("scores_done"), sem("top_step"), sem("bias_done")
        exp_done, inv_done, normed = sem("exp_done"), sem("inv_done"), sem("normed")
        prob_turned, probT_done = sem("prob_turned"), sem("probT_done")
        o_done, oT_done, out_done = sem("o_done"), sem("oT_done"), sem("out_done")
        yT_done, y_turned, x_updated = sem("yT_done"), sem("y_turned"), sem("x_updated")

        MOMENTS, TURN_XN, LOGITS, TURN_LOGITS, TURN_MIX = 3, 4, 5, 6, 9
        ROUTES = {6: range(0, 6), 7: range(6, 13), 8: range(13, ROUTE_STEPS)}

        def at(c, k):
            return STEPS * c + k, 2 * c + k // QUADS

        def row_tiles(b):
            return slice(b * TB, (b + 1) * TB) if isinstance(b, int) else bass.ds(b * TB, TB)

        def run(engine, engine_slot):
            for k in range(LEAD_A):
                engine_slot(0, k, False)
            with engine.Fori(0, NB // 2 - 1) as c:
                for k in range(LEAD_A, STEPS + LEAD_A):
                    engine_slot(c, k, False)
            for k in range(LEAD_A, STEPS + LEAD_A):
                engine_slot(NB // 2 - 1, k, True)

        block = ctx.enter_context(nc.Block())

        @block.tensor
        def _(pe):
            turn_row = rows.on_tensor(pe, v_bank)
            turn_chunk, logits, turn_logits, turn_mix = ahead.on_tensor(pe, o_bank)

            def turn_xn(c, k):
                s, b = at(c, k)
                pe.wait_ge(ln_step, LN_STEPS * (b + 1) + 3)
                pe.wait_ge(v_read, s + 1)
                turn_row()

            def project_qk(c, k, a, last):
                s, b = at(c, k)
                side, quad = k // QUADS % 2, k % QUADS
                xh, xl = xT_hi[:, side, :], xT_lo[:, side, :]
                if a == 0 and quad == 0:
                    pe.wait_ge(xT_lo_done, b + 1)
                if a == 0 and quad == 2 and k >= LEAD_A:
                    pe.wait_ge(x_updated, b)
                if a == 0 and quad == 3 and not (last and k == STEPS - 1):
                    pe.wait_ge(xT_lo_done, b + 2)
                if a == 0:
                    pe.wait_ge(v_read, s)
                elif not (isinstance(c, int) and c == 0 and k < 2):
                    pe.wait_ge(probT_done, 3 * s - 4)
                kind = ("pq", "pk")[a]
                for pair in range(2):
                    cols = slice((2 * quad + pair) * P, (2 * quad + pair + 1) * P)
                    o = (q_bank, k_bank)[a][:, pair * SEQ:(pair + 1) * SEQ]
                    hi, lo = w[kind + "_hi"][:, cols], w[kind + "_lo"][:, cols]
                    nc.tensor.matmul(o, hi, xh, start=True, stop=False)
                    nc.tensor.matmul(o, lo, xh, start=False, stop=False)
                    mm = nc.tensor.matmul(o, hi, xl, start=False, stop=True)
                mm.then_inc(proj_done, 1)

            def project_v(c, k):
                s, _ = at(c, k)
                side, quad = k // QUADS % 2, k % QUADS
                xh, xl = xT_hi[:, side, :], xT_lo[:, side, :]
                pe.wait_ge(q_read, s + 1)
                cols = slice(quad * 4 * HD, (quad + 1) * 4 * HD)
                hi, lo = w["pv_hi"][:, cols], w["pv_lo"][:, cols]
                for j in range(TB):
                    o = v_bank[:, j * SEQ:(j + 1) * SEQ]
                    t = slice(j * P, (j + 1) * P)
                    nc.tensor.matmul(o, xh[:, t], hi, start=True, stop=False)
                    nc.tensor.matmul(o, xh[:, t], lo, start=False, stop=False)
                    mm = nc.tensor.matmul(o, xl[:, t], hi, start=False, stop=True)
                mm.then_inc(proj_done, 1)

            def score_early(c, k):
                s, _ = at(c, k)
                i = k % 2
                pe.wait_ge(q_read, s + 1)
                pe.wait_ge(k_read, s + 1)
                pe.wait_ge(exp_done, 2 * s)
                for pair in range(2):
                    early = scores_early[:, pair * SEQ:(pair + 1) * SEQ]
                    nc.tensor.matmul(early, qT[:, i, pair, 0:P], kZ[:, i, pair, :, 0:P], start=True, stop=False)
                    mm = nc.tensor.matmul(early, w["ident_b"][:, :], w["mask"][:, :], start=False, stop=True)
                mm.then_inc(scores_done, 1)

            def score_late(c, k):
                i = k % 2
                for pair in range(2):
                    late = scores_late[pair]
                    nc.tensor.matmul(late[:, :], qT[:, i, pair, P:SEQ], kZ[:, i, pair, :, :], start=True, stop=False)
                    nc.tensor.matmul(late[:, :].rearrange("p (h n) -> p h n", h=2)[:, :, P:SEQ], w["ident_b"][:, :],
                                     w["mask"][:, :], start=False, stop=True).then_inc(scores_done, 1)

            def turn_prob(c, k, g, live):
                s, _ = at(c, k)
                pe.wait_ge(normed, 2 * s + (1 if g == 0 else 2))
                if g == 1 and live:
                    pe.wait_ge(k_read, s + 2)
                elif g == 2:
                    pe.wait_ge(probT_done, 3 * s + 1)
                elif not (isinstance(c, int) and c == 0 and k == 0):
                    pe.wait_ge(probT_done, 3 * s - g)
                bank = turn_bank[g]
                for j in range(4):
                    n = 4 * g + j
                    mm = nc.tensor.transpose(bank[:, j * P:(j + 1) * P], prob[:, n * P:(n + 1) * P],
                                             w["ident"][:, :])
                mm.then_inc(prob_turned, 1)

            def weigh_values(c, k, last):
                s, _ = at(c, k)
                i = k % 2
                pe.wait_ge(v_read, s + 1)
                pe.wait_ge(oT_done, s)
                if last and k + 1 == TURN_XN:
                    pe.wait_ge(ahead.xT_lo_done, 1)
                elif last and k + 1 in (LOGITS, TURN_LOGITS):
                    pe.wait_ge(ahead.score_done, k + 2 - LOGITS)
                for pair in range(2):
                    pe.wait_ge(probT_done, 3 * s + 2 + pair)
                    for kb in range(2):
                        for h in range(2):
                            hh = 2 * pair + h
                            cols = slice(hh * NPB + kb * SEQ, hh * NPB + (SEQ if kb == 0 else NPB))
                            mm = nc.tensor.matmul(o_bank[h * HD:(h + 1) * HD, pair * SEQ + kb * P:(pair + 1) * SEQ],
                                                  v[:, i, kb, hh * HD:(hh + 1) * HD], probT[:, cols],
                                                  start=(kb == 0), stop=(kb == 1))
                mm.then_inc(o_done, 1)

            def output(c, k):
                s, b = at(c, k)
                quad = k % QUADS
                pe.wait_ge(oT_done, s + 1)
                if quad == 0:
                    pe.wait_ge(yT_done, b)
                for pair in range(2):
                    n = 2 * quad + pair
                    mm = nc.tensor.matmul(acc[:, 0:SEQ], w["po"][:, n * P:(n + 1) * P],
                                          oT[:, k % 2, pair, :], start=(n == 0), stop=(n == 2 * QUADS - 1))
                mm.then_inc(out_done, 1)

            def turn_y(c, k, live):
                s, b = at(c, k)
                pe.wait_ge(yT_done, b)
                if live:
                    pe.wait_ge(v_read, s + 1)
                for j in range(TB):
                    mm = nc.tensor.transpose(v_bank[:, j * P:(j + 1) * P], yT[:, j * P:(j + 1) * P],
                                             w["ident"][:, :])
                mm.then_inc(y_turned, 1)

            def lead_in(c, k):
                s, _ = at(c, k)
                if k in (TURN_XN, LOGITS, TURN_LOGITS, TURN_MIX):
                    pe.wait_ge(oT_done, s - 1)
                if k == TURN_XN:
                    turn_chunk(0)
                elif k == LOGITS:
                    logits(0)
                elif k == TURN_LOGITS:
                    turn_logits(0)
                elif k == TURN_MIX:
                    turn_mix(0)

            def slot(c, k, last):
                live = k < STEPS or not last
                soft = k >= 1 and (k - 1 < STEPS or not last)
                if live:
                    project_qk(c, k, 0, last)
                    project_qk(c, k, 1, last)
                if k >= 2 and (k - 2 < STEPS or not last):
                    output(c, k - 2)
                if live:
                    project_v(c, k)
                if soft:
                    turn_prob(c, k - 1, 0, live)
                if last:
                    lead_in(c, k)
                if live:
                    score_early(c, k)
                if soft:
                    turn_prob(c, k - 1, 1, live)
                    turn_prob(c, k - 1, 2, live)
                if k % QUADS == 1 and k >= LEAD_A:
                    turn_y(c, k, live)
                if k % QUADS == 2 and not last:
                    turn_xn(c, k)
                if live:
                    score_late(c, k)
                if soft:
                    weigh_values(c, k - 1, last)

            run(pe, slot)

        @block.scalar
        def _(act):
            xT_high = rows.on_scalar(act, v_bank)
            chunk_high, sigmoid, copy_score, copy_mixT = ahead.on_scalar(act, o_bank)

            def exps(c, k):
                s, _ = at(c, k)
                i = k % 2
                if not (isinstance(c, int) and c == 0 and k < 1):
                    act.wait_ge(prob_turned, 3 * s)
                for pair in range(2):
                    act.wait_ge(bias_done, 2 * s + pair + 1)
                    early = scores_early[:, pair * SEQ:(pair + 1) * SEQ]
                    for h in range(2):
                        o = (2 * pair + h) * NPB
                        nc.scalar.activation(prob[:, o:o + P], early[:, h * P:(h + 1) * P], ACT.Exp,
                                             bias=bias[:, i, pair, 0, h:h + 1], scale=HD ** -0.5,
                                             accum_out=mass[:, i, pair, 0, h:h + 1])
                        e = nc.scalar.activation(prob[:, o + P:o + NPB],
                                                 scores_late[pair][:, h * SEQ:(h + 1) * SEQ], ACT.Exp,
                                                 bias=bias[:, i, pair, 1, h:h + 1], scale=HD ** -0.5,
                                                 accum_out=mass[:, i, pair, 1, h:h + 1])
                    e.then_inc(exp_done, 1)

            def copy_k(c, k):
                s, _ = at(c, k)
                if not (isinstance(c, int) and c == 0 and k < 2):
                    act.wait_ge(scores_done, 3 * s - 3)
                act.wait_ge(proj_done, 3 * s + 2)
                for h in range(2):
                    side_rows = slice(h * HD, (h + 1) * HD)
                    cp = nc.scalar.copy(kZ[side_rows, k % 2, :, h, :],
                                        k_bank[side_rows, :].rearrange("p (a n) -> p a n", a=2))
                cp.then_inc(k_read, 1)

            def copy_probT(c, k, last):
                s, _ = at(c, k)
                for g in range(3):
                    act.wait_ge(prob_turned, 3 * s + g + 1)
                    if g == 0:
                        act.wait_ge(o_done, s)
                    nc.scalar.copy(probT[:, g * 4 * P:(g + 1) * 4 * P],
                                   turn_bank[g][:, :]).then_inc(probT_done, 1)
                    if last and g == 0:
                        if k + 1 == TURN_XN:
                            chunk_high(0)
                        elif k + 1 == TURN_LOGITS:
                            copy_score(0)

            def copy_y(c, k):
                _, b = at(c, k)
                act.wait_ge(out_done, QUADS * b)
                nc.scalar.copy(yT[:, :], acc[:, 0:SEQ]).then_inc(yT_done, 1)

            def slot(c, k, last):
                soft = k >= 1 and (k - 1 < STEPS or not last)
                if soft:
                    exps(c, k - 1)
                if k < STEPS or not last:
                    copy_k(c, k)
                if k % QUADS == 1 and k >= LEAD_A:
                    copy_y(c, k)
                if soft:
                    copy_probT(c, k - 1, last)
                if last and k == LOGITS:
                    sigmoid(0)
                if last and k == TURN_MIX:
                    copy_mixT(0)
                if k % QUADS == 2 and not last:
                    xT_high(at(c, k)[1] + 1, (k // QUADS + 1) % 2)

            run(act, slot)

        @block.vector
        def _(dve):
            ln_moments, ln_apply, xT_low = rows.on_vector(dve, v_bank)
            chunk_moments, chunk_apply, chunk_low, route = ahead.on_vector(dve, o_bank)

            def copy_q(c, k):
                s, _ = at(c, k)
                if not (isinstance(c, int) and c == 0 and k < 2):
                    dve.wait_ge(scores_done, 3 * s - 3)
                dve.wait_ge(proj_done, 3 * s + 1)
                nc.vector.tensor_copy(qT[:, k % 2, :, :], q_bank[:, :].rearrange("p (a n) -> p a n", a=2))\
                    .then_inc(q_read, 1)

            def copy_v(c, k):
                s, _ = at(c, k)
                if not (isinstance(c, int) and c == 0 and k < 2):
                    dve.wait_ge(o_done, s - 1)
                dve.wait_ge(proj_done, 3 * s + 3)
                nc.vector.tensor_copy(v[:, k % 2, :, :], v_bank[:, :].rearrange("p (a n) -> p a n", a=TB))\
                    .then_inc(v_read, 1)

            def normalise(c, k, pair):
                s, _ = at(c, k)
                i = k % 2
                dve.wait_ge(exp_done, 2 * s + pair + 1)
                nc.vector.reciprocal(inv[:, i, pair, :, :], mass[:, i, pair, :, :]).then_inc(inv_done, 1)
                dve.wait_ge(inv_done, 2 * s + pair + 1)
                for h in range(2):
                    o = (2 * pair + h) * NPB
                    for late, (a, b) in enumerate(((o, o + P), (o + P, o + NPB))):
                        m = nc.vector.tensor_scalar(prob[:, a:b], prob[:, a:b],
                                                    inv[:, i, pair, late, h:h + 1], None, ALU.mult)
                m.then_inc(normed, 1)

            def copy_o(c, k):
                s, _ = at(c, k)
                if not (isinstance(c, int) and c == 0 and k < 2):
                    dve.wait_ge(out_done, s - 1)
                dve.wait_ge(o_done, s + 1)
                nc.vector.tensor_copy(oT[:, k % 2, :, :], o_bank[:, :].rearrange("p (a n) -> p a n", a=2))\
                    .then_inc(oT_done, 1)

            def maxima(c, k):
                s, _ = at(c, k)
                i = k % 2
                dve.wait_ge(scores_done, 3 * s + 1)
                early = scores_early[:, :].rearrange("p (a h n) -> p a h n", a=2, h=2)
                nc.vector.tensor_reduce(top[:, i, :, 0, :], early, AX_X, ALU.max)
                for pair in range(2):
                    dve.wait_ge(scores_done, 3 * s + pair + 2)
                    late = scores_late[pair][:, :].rearrange("p (h n) -> p h n", h=2)
                    nc.vector.tensor_reduce(top[:, i, pair, 1, :], late, AX_X, ALU.max).then_inc(top_step, 1)
                    dve.wait_ge(top_step, 2 * s + pair + 1)
                    nc.vector.tensor_scalar(bias[:, i, pair, :, :], top[:, i, pair, :, :], -HD ** -0.5, None,
                                            ALU.mult).then_inc(bias_done, 1)

            def update_x(c, k):
                _, b = at(c, k)
                dve.wait_ge(y_turned, b)
                t = x_all[:, row_tiles(b - 1), :].rearrange("p t d -> p (t d)")
                nc.vector.tensor_tensor(t, v_bank[:, 0:SEQ], t, ALU.add).then_inc(x_updated, 1)

            def slot(c, k, last):
                live = k < STEPS or not last
                soft = k >= 1 and (k - 1 < STEPS or not last)
                b = at(c, k)[1]
                if k >= 2 and (k - 2 < STEPS or not last):
                    copy_o(c, k - 2)
                if live:
                    copy_q(c, k)
                if soft:
                    normalise(c, k - 1, 0)
                    normalise(c, k - 1, 1)
                if last and k == MOMENTS:
                    chunk_moments(0)
                if k % QUADS == 1 and not last:
                    ln_moments(b + 1)
                if k % QUADS == 2 and not last:
                    ln_apply(b + 1)
                if live:
                    copy_v(c, k)
                if last and k == MOMENTS:
                    chunk_apply(0)
                if last and k == TURN_XN:
                    chunk_low(0)
                if k % QUADS == 1 and k >= LEAD_A:
                    update_x(c, k)
                if k % QUADS == 2 and not last:
                    xT_low(b + 1, (k // QUADS + 1) % 2)
                if live:
                    maxima(c, k)
                if last:
                    for i in ROUTES.get(k, ()):
                        route(0, i)

            for i in range(2):
                for h in range(2):
                    side_rows = slice((1 - h) * HD, (2 - h) * HD)
                    nc.vector.memset(kZ[side_rows, i, :, h, :], 0.0)
            run(dve, slot)

        @block.gpsimd
        def _(pool):
            rstd_of = rows.on_gpsimd(pool)
            with pool.Fori(1, NB) as n:
                rstd_of(n)
            ahead.on_gpsimd(pool)(0)

        @block.sync
        def _(sp):
            ahead.on_sync(sp)(0)


def macaron(nc, x, P_q, P_k, P_v, P_o, gate_w, gate_bias, We_gate, We_up, We_down, Ws_gate, Ws_up, Ws_down, out):
    B, M, _ = x.shape
    tiles = B * M // P
    dr = {"pq": P_q, "pk": P_k, "pv": P_v, "po": P_o, "gw": gate_w, "wg": We_gate, "wu": We_up, "wd": We_down,
          "sg": Ws_gate, "su": Ws_up, "sd": Ws_down,
          "gb": gate_bias.rearrange("(a e) -> a e", a=1).to_broadcast([P, E])}
    x_v = x.rearrange("b (t p) d -> p (b t) d", p=P)
    out_v = out.rearrange("b (t p) d -> p (b t) d", p=P)
    mix_rows = nc.dram_tensor("mix_rows", (tiles // CT, E, CHUNK), F32, kind="Internal").ap()
    with ExitStack() as ctx:
        def sb(name, shape, dt=F32):
            return ctx.enter_context(nc.sbuf_tensor(name, shape, dt))

        x_all = sb("x_all", [P, tiles, D])
        w = {}
        for kind in ("wg", "wu", "wd"):
            for part in ("_hi", "_lo"):
                w[kind + part] = sb(kind + part, [P, SLOTS * P], F32R)
        with nc.sbuf_tensor("landing", [P, LANDINGS, H * HD], F32) as landing:
            w["landing"] = landing
        for kind in ("pq", "pk", "pv"):
            for part in ("_hi", "_lo"):
                w[kind + part] = sb(kind + part, [P, H * HD], F32R)
        w["po"] = sb("po", [P, H * HD])
        w["gw_hi"], w["gw_lo"] = sb("gw_hi", [P, P], F32R), sb("gw_lo", [P, P], F32R)
        w["bias"] = sb("gate_bias", [P, E])
        w["ident"] = sb("ident", [P, P])
        w["ident_b"] = sb("ident_b", [P, P], BF16)
        w["mask"] = sb("mask", [P, 2 * P], BF16)
        w["earlier"] = sb("earlier", [P, E])
        w["minus_half"] = sb("minus_half", [P, CT])
        w["eps"] = sb("eps", [P, CT])
        psum = [ctx.enter_context(nc.psum_tensor(f"bank{i}", [P, 512], F32)) for i in range(8)]

        b = router_buffers(ctx, nc)
        first, second = (router(ctx, nc, tag, w, x_all, mix_rows, b) for tag in ("r1_", "r2_"))

        rows = row_norm(ctx, nc, w, x_all)

        ffn(nc, "f1_", w, x_all, psum, mix_rows, b, first, rows=rows, load=(x_v, dr))
        attention(nc, w, x_all, psum, rows, second)
        ffn(nc, "f2_", w, x_all, psum, mix_rows, b, second, out=out_v)


_INS = ["L0_attn_x", "L0_attn_P_q", "L0_attn_P_k", "L0_attn_P_v", "L0_attn_P_o", "L0_ffn_gate_w", "L0_ffn_gate_bias",
        "L0_ffn_We_gate", "L0_ffn_We_up", "L0_ffn_We_down", "L0_ffn_Ws_gate", "L0_ffn_Ws_up", "L0_ffn_Ws_down"]


def kernel(**inputs):
    import numpy as _np
    import concourse.bacc as _bacc
    from concourse import mybir as _mybir
    from concourse.bass_utils import run_bass_kernel_spmd as _run

    nc = _bacc.Bacc("TRN2", target_bir_lowering=False, num_devices=1)
    arrays, args = {}, []
    for name in _INS:
        a = _np.ascontiguousarray(inputs[name])
        arrays[f"in_{name}"] = a
        args.append(nc.dram_tensor(f"in_{name}", a.shape, _mybir.dt.from_np(a.dtype), kind="ExternalInput").ap())
    x = arrays["in_L0_attn_x"]
    out = nc.dram_tensor("out_0", x.shape, _mybir.dt.from_np(x.dtype), kind="ExternalOutput").ap()
    macaron(nc, *args, out)
    r = _run(nc, [arrays], core_ids=[0])
    return r.results[0]["out_0"]
```
